# Optimizing a Trainium2 kernel written in Bass

```python
import numpy as np
import jax
import jax.numpy as jnp

def _softmax(x, axis=-1):
    return jax.nn.softmax(x, axis=axis)

def _gelu(x):
    return jax.nn.gelu(x, approximate=True)

def _silu(x):
    return jax.nn.silu(x)

def _sigmoid(x):
    return jax.nn.sigmoid(x)

def _layernorm(x, axis=-1, eps=1e-05):
    m = jnp.mean(x, axis=axis, keepdims=True)
    v = jnp.var(x, axis=axis, keepdims=True)
    return (x - m) / jnp.sqrt(v + eps)

def _scatter_add(tgt, idx, src, axis=0):
    return tgt.at[idx].add(src)

def _segment_sum(src, seg, n):
    return jax.ops.segment_sum(src, seg, n)
kernel_name = 'mk_macaron_d1_jaxref_r8_4f3afa'

def setup_inputs(seed: int=0):
    np.random.seed(seed)
    _w = jnp.asarray

    def _L0_attn_setup():
        import jax, jax.numpy as jnp
        import numpy as np
        B, N, HID = (1, 256, 512)
        H, KVH, D, W = (32, 8, 128, 64)
        THETA = 10000.0
        GATE_NORM = 16.0

        def rope(x, pos):
            half = jnp.arange(D // 2, dtype=jnp.float32)
            inv = 1.0 / THETA ** (2.0 * half / D)
            fr = pos[:, None].astype(jnp.float32) * inv[None, :]
            emb = jnp.concatenate([fr, fr], axis=-1)
            cos, sin = (jnp.cos(emb)[None, None], jnp.sin(emb)[None, None])
            x1, x2 = jnp.split(x, 2, axis=-1)
            rot = jnp.concatenate([-x2, x1], axis=-1)
            return x * cos + rot * sin

        def gla_scan(q, k, v, g):
            qt, kt, vt, gt = (jnp.moveaxis(t, 2, 0) for t in (q, k, v, g))
            b, h = (q.shape[0], q.shape[1])
            S0 = jnp.zeros((b, h, D, D), jnp.float32)

            def step(S, x):
                q_t, k_t, v_t, g_t = x
                S = S * jnp.exp(g_t)[..., None] + k_t[..., None] * v_t[..., None, :]
                return (S, jnp.einsum('bhk,bhkv->bhv', q_t, S))
            _, o = jax.lax.scan(step, S0, (qt, kt, vt, gt))
            return jnp.moveaxis(o, 0, 2)

        def sliding_window_attn(q, k, v):
            b, h, n, d = q.shape
            nb = n // W
            qb = q.reshape(b, h, nb, W, d)

            def two_blocks(x):
                xb = x.reshape(b, h, nb, W, d)
                prev = jnp.concatenate([jnp.zeros_like(xb[:, :, :1]), xb[:, :, :-1]], axis=2)
                return jnp.concatenate([prev, xb], axis=3)
            kb, vb = (two_blocks(k), two_blocks(v))
            scores = jnp.einsum('bhnqd,bhnkd->bhnqk', qb, kb) / jnp.sqrt(jnp.float32(d))
            a = jnp.arange(W)[:, None]
            c = jnp.arange(2 * W)[None, :]
            rel = a + W - c
            base = (rel >= 0) & (rel <= W)
            blk = jnp.arange(nb)[:, None, None]
            keypos = (blk - 1) * W + c[None]
            mask = base[None] & (keypos >= 0)
            scores = jnp.where(mask[None, None], scores, -jnp.inf)
            p = jax.nn.softmax(scores, axis=-1)
            ob = jnp.einsum('bhnqk,bhnkd->bhnqd', p, vb)
            return ob.reshape(b, h, n, d)
        key = jax.random.key(seed)
        ks = jax.random.split(key, 5)
        s = 0.02
        return {'hidden_states': jax.random.normal(ks[0], (B, N, HID), jnp.float32), 'Wq': jax.random.normal(ks[1], (HID, H * D), jnp.float32) * s, 'Wk': jax.random.normal(ks[2], (HID, KVH * D), jnp.float32) * s, 'Wv': jax.random.normal(ks[3], (HID, KVH * D), jnp.float32) * s, 'Wo': jax.random.normal(ks[4], (H * D, HID), jnp.float32) * s}
    _L0_attn_in = _L0_attn_setup()

    def _L0_ffn_setup():
        import jax, jax.numpy as jnp
        import numpy as np
        B, S, DIN, DOUT, R = (2, 256, 512, 512, 32)
        key = jax.random.key(seed)
        k1, k2, k3, k4, k5 = jax.random.split(key, 5)
        std = 1.0 / np.sqrt(R)
        return {'x': jax.random.normal(k1, (B, S, DIN), dtype=jnp.float32), 'W': jax.random.normal(k2, (DOUT, DIN), dtype=jnp.float32) * 0.02, 'lora_A': jax.random.normal(k3, (R, DIN), dtype=jnp.float32) * std, 'lora_B': jax.random.normal(k4, (DOUT, R), dtype=jnp.float32) * 0.01, 'magnitude': jax.random.uniform(k5, (DOUT,), dtype=jnp.float32) + 0.5}
    _L0_ffn_in = _L0_ffn_setup()
    _d = {'L0_attn_hidden_states': _L0_attn_in['hidden_states'], 'L0_attn_Wq': _L0_attn_in['Wq'], 'L0_attn_Wk': _L0_attn_in['Wk'], 'L0_attn_Wv': _L0_attn_in['Wv'], 'L0_attn_Wo': _L0_attn_in['Wo'], 'L0_ffn_W': _L0_ffn_in['W'], 'L0_ffn_lora_A': _L0_ffn_in['lora_A'], 'L0_ffn_lora_B': _L0_ffn_in['lora_B'], 'L0_ffn_magnitude': _L0_ffn_in['magnitude']}
    _x0 = _d['L0_attn_hidden_states']
    _d['L0_attn_hidden_states'] = jax.random.normal(jax.random.fold_in(jax.random.key(seed), 1), (4, 256, 512), dtype=_x0.dtype)
    del _x0
    return _d

def reference(L0_attn_hidden_states, L0_attn_Wq, L0_attn_Wk, L0_attn_Wv, L0_attn_Wo, L0_ffn_W, L0_ffn_lora_A, L0_ffn_lora_B, L0_ffn_magnitude):

    def _L0_attn_ref(hidden_states, Wq, Wk, Wv, Wo):
        import jax, jax.numpy as jnp
        import numpy as np
        B, N, HID = (1, 256, 512)
        H, KVH, D, W = (32, 8, 128, 64)
        THETA = 10000.0
        GATE_NORM = 16.0

        def rope(x, pos):
            half = jnp.arange(D // 2, dtype=jnp.float32)
            inv = 1.0 / THETA ** (2.0 * half / D)
            fr = pos[:, None].astype(jnp.float32) * inv[None, :]
            emb = jnp.concatenate([fr, fr], axis=-1)
            cos, sin = (jnp.cos(emb)[None, None], jnp.sin(emb)[None, None])
            x1, x2 = jnp.split(x, 2, axis=-1)
            rot = jnp.concatenate([-x2, x1], axis=-1)
            return x * cos + rot * sin

        def gla_scan(q, k, v, g):
            qt, kt, vt, gt = (jnp.moveaxis(t, 2, 0) for t in (q, k, v, g))
            b, h = (q.shape[0], q.shape[1])
            S0 = jnp.zeros((b, h, D, D), jnp.float32)

            def step(S, x):
                q_t, k_t, v_t, g_t = x
                S = S * jnp.exp(g_t)[..., None] + k_t[..., None] * v_t[..., None, :]
                return (S, jnp.einsum('bhk,bhkv->bhv', q_t, S))
            _, o = jax.lax.scan(step, S0, (qt, kt, vt, gt))
            return jnp.moveaxis(o, 0, 2)

        def sliding_window_attn(q, k, v):
            b, h, n, d = q.shape
            nb = n // W
            qb = q.reshape(b, h, nb, W, d)

            def two_blocks(x):
                xb = x.reshape(b, h, nb, W, d)
                prev = jnp.concatenate([jnp.zeros_like(xb[:, :, :1]), xb[:, :, :-1]], axis=2)
                return jnp.concatenate([prev, xb], axis=3)
            kb, vb = (two_blocks(k), two_blocks(v))
            scores = jnp.einsum('bhnqd,bhnkd->bhnqk', qb, kb) / jnp.sqrt(jnp.float32(d))
            a = jnp.arange(W)[:, None]
            c = jnp.arange(2 * W)[None, :]
            rel = a + W - c
            base = (rel >= 0) & (rel <= W)
            blk = jnp.arange(nb)[:, None, None]
            keypos = (blk - 1) * W + c[None]
            mask = base[None] & (keypos >= 0)
            scores = jnp.where(mask[None, None], scores, -jnp.inf)
            p = jax.nn.softmax(scores, axis=-1)
            ob = jnp.einsum('bhnqk,bhnkd->bhnqd', p, vb)
            return ob.reshape(b, h, n, d)
        b, n, _ = hidden_states.shape
        grp = H // KVH
        q = hidden_states @ Wq
        k = hidden_states @ Wk
        v = hidden_states @ Wv
        g = k
        q = q.reshape(b, n, H, D).transpose(0, 2, 1, 3)
        k = k.reshape(b, n, KVH, D).transpose(0, 2, 1, 3)
        v = v.reshape(b, n, KVH, D).transpose(0, 2, 1, 3)
        g = g.reshape(b, n, KVH, D).transpose(0, 2, 1, 3)
        k = jnp.repeat(k, grp, axis=1)
        v = jnp.repeat(v, grp, axis=1)
        g = jnp.repeat(g, grp, axis=1)
        sq, sk, sv = (q, k, v)
        qs = jax.nn.softmax(q.astype(jnp.float32), axis=-1)
        ks_ = jax.nn.softmax(k.astype(jnp.float32), axis=-1)
        gs = jax.nn.log_sigmoid(g.astype(jnp.float32)) / GATE_NORM
        o_lin = gla_scan(qs, ks_, v.astype(jnp.float32), gs)
        pos = jnp.arange(n)
        sq = rope(sq, pos)
        sk = rope(sk, pos)
        y = sliding_window_attn(sq, sk, sv)
        o_ = 0.5 * y + 0.5 * o_lin
        o_ = o_.astype(jnp.bfloat16).astype(jnp.float32)
        o = o_.transpose(0, 2, 1, 3).reshape(b, n, H * D) @ Wo
        return o

    def _L0_ffn_ref(x, W, lora_A, lora_B, magnitude):
        import jax, jax.numpy as jnp
        import numpy as np
        B, S, DIN, DOUT, R = (2, 256, 512, 512, 32)
        base = jnp.einsum('bsi,oi->bso', x, W)
        lora = jnp.einsum('bsr,or->bso', jnp.einsum('bsi,ri->bsr', x, lora_A), lora_B)
        eff_W = W + lora_B @ lora_A
        column_norm = jax.lax.stop_gradient(jnp.sqrt(jnp.sum(eff_W * eff_W, axis=1)))
        result = (base + lora) / column_norm[None, None, :]
        return result * magnitude[None, None, :]
    x = L0_attn_hidden_states
    x = x + 0.5 * _L0_ffn_ref(_layernorm(x, axis=-1), L0_ffn_W, L0_ffn_lora_A, L0_ffn_lora_B, L0_ffn_magnitude)
    x = x + _L0_attn_ref(_layernorm(x, axis=-1), L0_attn_Wq, L0_attn_Wk, L0_attn_Wv, L0_attn_Wo)
    x = x + 0.5 * _L0_ffn_ref(_layernorm(x, axis=-1), L0_ffn_W, L0_ffn_lora_A, L0_ffn_lora_B, L0_ffn_magnitude)
    return x

_drawn_inputs = setup_inputs


def setup_inputs(seed=0):
    import zlib

    import numpy as np

    out = dict(_drawn_inputs(seed))
    spreads = {}
    factors = {'L0_attn_Wq': 8.0, 'L0_attn_Wk': 8.0}
    for name, (base, spread) in spreads.items():
        noise = np.random.default_rng([zlib.crc32(name.encode()), seed]).standard_normal(out[name].shape)
        drawn = base * np.exp(spread * noise) if base else spread * noise
        out[name] = jnp.asarray(drawn.astype(out[name].dtype))
    for name, factor in factors.items():
        out[name] = (out[name] * factor).astype(out[name].dtype)
    return out
```

```python
from contextlib import ExitStack

import concourse.bass as bass
from concourse import mybir

P = 128
B, N, HID = 4, 256, 512
H, KVH, D, W = 32, 8, 128, 64
R = 32
GRP = H // KVH
HEADS = GRP + 1
KT = HID // P
TOK = B * N // P
TT = N // P
NB = N // W
QW = GRP * D
UNITS = KVH * B
EPS = 1e-5
GATE_NORM = 16.0
MOST = 85.0 * GATE_NORM
FAR = -1.0e30
BIG = 3.0e38

F32 = mybir.dt.float32
F32R = mybir.dt.float32r
BF16 = mybir.dt.bfloat16
ALU = mybir.AluOpType
ACT = mybir.ActivationFunctionType
AX_X = mybir.AxisListType.X

KEYS = 5
DQ = KEYS * P
DSTEP = DQ + N
LIN_KEYS = (0, 1, 3, 4)
STATE_KEYS = 2

C_COS, C_SIN, C_WIN, C_LIN, C_ID, C_ONE = 0, TT * D, 2 * TT * D, 2 * TT * D + 3 * P, 2 * TT * D + 5 * P, 2 * TT * D + 6 * P
C_ALL = C_ONE + N
SPLIT_AT = ((0,), (1,), (2, 3), ())
WIN_OF_BLOCK = (0, 1, 2, 1)


def layer_program(nc, hs, wq, wk, wv, wo, fw, la, lb, mag, consts, out):
    ctx = ExitStack()
    with ctx:
        def sb(name, shape, dt=F32):
            return ctx.enter_context(nc.sbuf_tensor(name, shape, dt))

        def sem(name):
            return ctx.enter_context(nc.semaphore(name))

        def sems(name, n=2):
            return [sem(f"{name}{i}") for i in range(n)]

        x = sb("x", [P, TOK, HID])
        xt_hi = sb("xt_hi", [P, KT, TOK * P], F32R)
        xt_lo = sb("xt_lo", [P, KT, TOK * P], F32R)
        w_hi = [sb(f"w_hi{i}", [P, KT, QW + 2 * D], F32R) for i in range(2)]
        w_lo = [sb(f"w_lo{i}", [P, KT, QW + 2 * D], F32R) for i in range(2)]
        w_raw = [sb(f"w_raw{i}", [P, QW + 2 * D]) for i in range(2)]
        wo_hi = sb("wo_hi", [P, GRP, HID], F32R)
        wo_lo = sb("wo_lo", [P, GRP, HID], F32R)
        wo_raw = sb("wo_raw", [P, GRP, HID])
        fwt = sb("fwt", [P, KT, HID])
        cst = sb("cst", [P, C_ALL])
        qk = [sb(f"qk{i}", [P, HEADS, D]) for i in range(TT)]
        rc = [sb(f"rc{i}", [P, HEADS, D]) for i in range(TT)]
        rs = [sb(f"rs{i}", [P, HEADS, D]) for i in range(TT)]
        es = [sb(f"es{i}", [P, HEADS, D]) for i in range(TT)]
        v = [sb(f"v{i}", [P, TT, D]) for i in range(2)]
        vmix = sb("vmix", [P, D])
        krawT = sb("krawT", [P, N])
        krT = sb("krT", [P, N])
        ksT = sb("ksT", [P, N])
        lnk = sb("lnk", [P, N])
        logs = sb("logs", [P, N])
        G = sb("G", [P, N])
        dec = sb("dec", [P, DSTEP + 1])
        kg = sb("kg", [P, KEYS, P])
        qrT = sb("qrT", [P, NB, GRP, W])
        qg = sb("qg", [P, NB, GRP, W])
        k2 = sb("k2", [P, D])
        state = sb("state", [P, 2, D])
        sc = sb("sc", [P, 8, P])
        mix = sb("mix", [P, 8, P])
        mT = sb("mT", [P, 8, P])
        o_bf = sb("o_bf", [P, TT, GRP, P], BF16)
        o_r = sb("o_r", [P, TT, GRP, P], F32R)
        nmax = [sb(f"nmax{i}", [P, HEADS]) for i in range(TT)]
        esum = [sb(f"esum{i}", [P, HEADS]) for i in range(TT)]
        erec = [sb(f"erec{i}", [P, HEADS]) for i in range(TT)]
        scmin = sb("scmin", [P, 8])
        ssum = sb("ssum", [P, 8])
        srec = sb("srec", [P, 8])
        stat = [sb(f"stat{i}", [P, 6]) for i in range(2)]
        meanvar = [sb(f"meanvar{i}", [P, 2]) for i in range(2)]
        dev = [sb(f"dev{i}", [P, 1]) for i in range(2)]
        rstd = [sb(f"rstd{i}", [P, 1]) for i in range(2)]
        magc = sb("magc", [P, KT])
        norm2 = sb("norm2", [P, KT])
        colscale = sb("colscale", [P, KT])
        xn = [sc[:, 0:4, :].rearrange("p a b -> p (a b)"), sc[:, 4:8, :].rearrange("p a b -> p (a b)")]
        eff = wo_raw
        squares = mix[:, 0:4, :].rearrange("p a b -> p (a b)")
        lbT = mT[0:R, 0:4, :].rearrange("p a b -> p (a b)")
        la_sb = mT[0:R, 4:8, :].rearrange("p a b -> p (a b)")
        lb_sb = k2[:, :].rearrange("p (c r) -> p c r", r=R)

        cos = cst[:, C_COS:C_SIN].rearrange("p (t d) -> p t d", d=D)
        sin = cst[:, C_SIN:C_WIN].rearrange("p (t d) -> p t d", d=D)
        win = cst[:, C_WIN:C_LIN].rearrange("p (n k) -> p n k", k=P)
        lin = cst[:, C_LIN:C_ID].rearrange("p (n k) -> p n k", k=P)
        ident = cst[:, C_ID:C_ONE]
        ones = cst[:, C_ONE:C_ALL]

        bank = [ctx.enter_context(nc.psum_tensor(f"bank{i}", [P, 512], F32)) for i in range(8)]
        q_bank, kv_bank = bank[0], bank[1]
        turn_bank = bank[2:4]
        score_bank = bank[4:6]
        lin_bank = bank[6:8]

        x_in = sems("x_in", TOK)
        cst_in, fw_in, lora_in = sem("cst_in"), sem("fw_in"), sem("lora_in")
        lb_turned, lb_copied, ba_made, eff_made = sem("lb_turned"), sem("lb_copied"), sem("ba_made"), sem("eff_made")
        squared, rooted, scaled_c, eff_scaled = sem("squared"), sem("rooted"), sem("scaled_c"), sem("eff_scaled")
        fwt_turned, fwt_copied = sem("fwt_turned"), sem("fwt_copied")
        fw_hi_ready, fw_lo_ready = sem("fw_hi_ready"), sem("fw_lo_ready")
        stats_made, dev_made, rstd_made = sem("stats_made"), sem("dev_made"), sem("rstd_made")
        xn_made, xn_turned, xt_hi_made, xt_lo_made = sem("xn_made"), sem("xn_turned"), sem("xt_hi_made"), sem("xt_lo_made")
        ffn_made, ffn_added, stored = sem("ffn_made"), sem("ffn_added"), sem("stored")

        w_in = sems("w_in")
        wo_in = sem("wo_in")
        w_hi_ready, w_lo_ready = sem("w_hi_ready"), sem("w_lo_ready")
        wo_hi_ready, wo_lo_ready = sem("wo_hi_ready"), sem("wo_lo_ready")

        q_made, kv_made = sems("q_made"), sems("kv_made")
        q_copied, kv_copied = sems("q_copied"), sems("kv_copied")
        max_made, rotated, roped = sems("max_made"), sems("rotated"), sems("roped")
        es_made, es_recip, es_scaled = sems("es_made"), sems("es_recip"), sems("es_scaled")
        v_mixed = sem("v_mixed")
        kraw_turned, kr_turned, ks_turned = sem("kraw_turned"), sem("kr_turned"), sem("ks_turned")
        kraw_copied, kr_copied, ks_copied = sem("kraw_copied"), sem("kr_copied"), sem("ks_copied")
        qr_turned, qr_copied, es_turned = sems("qr_turned"), sems("qr_copied"), sems("es_turned")
        abs_made, kexp_made, kln_made = sem("abs_made"), sem("kexp_made"), sem("kln_made")
        logs_made, summed, dec_made, dec_bounded, gates_made = (
            sem("logs_made"), sem("summed"), sem("dec_made"), sem("dec_bounded"), sem("gates_made"))
        kg_made, qg_made = sem("kg_made"), sems("qg_made")
        k2_turned, k2_copied, state_made, state_copied = (
            sem("k2_turned"), sem("k2_copied"), sem("state_made"), sem("state_copied"))
        scored, masked, e_made, e_recip = sems("scored"), sems("masked"), sems("e_made"), sems("e_recip")
        lin_made, lin_masked, mixed = sems("lin_made"), sems("lin_masked"), sems("mixed")
        m_turned, m_copied, pv_made, o_copied, o_ready = (
            sems("m_turned"), sems("m_copied"), sems("pv_made"), sems("o_copied"), sems("o_ready"))
        out_made, out_added = sems("out_made"), sems("out_added")

        BEFORE = [(r, i - 2 * r) for i in range(TOK + 2) for r in (0, 1) if 0 <= i - 2 * r < TOK]
        NORMS = BEFORE + [(2, i) for i in range(TOK)]
        number = {norm: n for n, norm in enumerate(NORMS)}

        def over_units(eng, step):
            for b in range(B):
                step(0, b, first=b == 0, last=False)
            with eng.Fori(1, KVH - 1, 2) as g:
                for b in range(B):
                    step(g, b, first=False, last=False, odd=True)
                for b in range(B):
                    step(g + 1, b, first=False, last=False)
            for b in range(B):
                step(KVH - 1, b, first=False, last=b == B - 1, odd=True, last_group=True)

        block = ctx.enter_context(nc.Block())

        @block.sync
        def _(sp):
            sp.dma_start(cst[:, :], consts).then_inc(cst_in, 16)
            sp.dma_start(lb_sb, lb.rearrange("(c p) r -> p c r", p=P)).then_inc(lora_in, 16)
            sp.dma_start(la_sb, la).then_inc(lora_in, 16)
            sp.dma_start(fwt[:, :, :], fw.rearrange("(c p) i -> p c i", p=P)).then_inc(fw_in, 16)
            sp.dma_start(magc[:, :], mag).then_inc(fw_in, 16)
            for i in range(TOK):
                sp.dma_start(x[:, i, :], hs[i * P:(i + 1) * P, :]).then_inc(x_in[i], 16)

            def load_chunk(g, k):
                s = k % 2
                rows = slice(k * P, (k + 1) * P)
                sp.dma_start(w_raw[s][:, 0:QW], wq[rows, bass.ds(g * QW, QW)]).then_inc(w_in[s], 16)
                sp.dma_start(w_raw[s][:, QW:QW + D], wk[rows, bass.ds(g * D, D)]).then_inc(w_in[s], 16)
                sp.dma_start(w_raw[s][:, QW + D:], wv[rows, bass.ds(g * D, D)]).then_inc(w_in[s], 16)

            for k in range(KT):
                if k >= 2:
                    sp.wait_ge(w_hi_ready, k - 1)
                    sp.wait_ge(w_lo_ready, k - 1)
                load_chunk(0, k)
            sp.wait_ge(eff_scaled, KT)
            sp.wait_ge(fwt_turned, KT)
            sp.dma_start(wo_raw[:, :, :], wo[0:QW, :].rearrange("(h d) n -> d h n", d=D)).then_inc(wo_in, 16)
            with sp.Fori(1, KVH) as g:
                for k in range(KT):
                    sp.wait_ge(w_hi_ready, g * KT + (k - 1))
                    sp.wait_ge(w_lo_ready, g * KT + (k - 1))
                    load_chunk(g, k)
                    if k == 1:
                        sp.wait_ge(wo_hi_ready, g)
                        sp.wait_ge(wo_lo_ready, g)
                        sp.dma_start(wo_raw[:, :, :], wo[bass.ds(g * QW, QW), :].rearrange("(h d) n -> d h n", d=D))\
                          .then_inc(wo_in, 16)
            for i in range(TOK):
                sp.wait_ge(ffn_added, TOK + i + 1)
                sp.dma_start(out[i * P:(i + 1) * P, :], x[:, i, :]).then_inc(stored, 16)
            sp.wait_ge(stored, 16 * TOK)

        @block.tensor
        def _(pe):
            def three(dst, a_hi, a_lo, b_hi, b_lo, start, stop):
                pe.matmul(dst, a_hi, b_hi, start=start, stop=False)
                pe.matmul(dst, a_hi, b_lo, start=False, stop=False)
                return pe.matmul(dst, a_lo, b_hi, start=False, stop=stop)

            def turn_norm(n):
                pe.wait_ge(xn_made, n + 1)
                if n >= 2:
                    pe.wait_ge(xt_lo_made, n - 1)
                for k in range(KT):
                    t = pe.transpose(turn_bank[n % 2][:, k * P:(k + 1) * P], xn[n % 2][:, k * P:(k + 1) * P], ident)
                t.then_inc(xn_turned, 1)

            def ffn(f):
                i = f % TOK
                pe.wait_ge(xt_hi_made, number[(2 * (f // TOK), i)] + 1)
                pe.wait_ge(xt_lo_made, number[(2 * (f // TOK), i)] + 1)
                if f >= 2:
                    pe.wait_ge(ffn_added, f - 1)
                for k in range(KT):
                    cols = slice(i * P, (i + 1) * P)
                    mm = three(score_bank[f % 2][:, :], xt_hi[:, k, cols], xt_lo[:, k, cols],
                               wo_hi[:, k, :], wo_lo[:, k, :], k == 0, k == KT - 1)
                mm.then_inc(ffn_made, 1)

            pe.wait_ge(cst_in, 16)
            pe.wait_ge(lora_in, 32)
            for c in range(KT):
                t = pe.transpose(bank[0][0:R, c * P:(c + 1) * P], lb_sb[:, c, :], ident)
            t.then_inc(lb_turned, 1)
            pe.wait_ge(lb_copied, 1)
            for c in range(KT):
                pe.matmul(bank[4 + c][:, :], lbT[:, c * P:(c + 1) * P], la_sb, start=True, stop=True).then_inc(ba_made, 1)
            for c in range(KT):
                pe.wait_ge(eff_scaled, c + 1)
                for k in range(KT):
                    t = pe.transpose(bank[k][:, c * P:(c + 1) * P], eff[:, c, k * P:(k + 1) * P], ident)
                t.then_inc(fwt_turned, 1)
            pe.wait_ge(fwt_copied, KT)
            for i in range(TOK + 3):
                if i < TOK:
                    turn_norm(number[(0, i)])
                if i == 1:
                    pe.wait_ge(fw_hi_ready, 1)
                    pe.wait_ge(fw_lo_ready, 1)
                if 0 <= i - 2 < TOK:
                    turn_norm(number[(1, i - 2)])
                if 0 <= i - 1 < TOK:
                    ffn(i - 1)

            def project(u, b, tile, wpar, new_weights, first=False):
                if new_weights is not None:
                    pe.wait_ge(w_hi_ready, new_weights)
                    pe.wait_ge(w_lo_ready, new_weights)
                i = b * TT + tile
                cols = slice(i * P, (i + 1) * P)
                if first and tile == 0:
                    pe.wait_ge(xt_hi_made, 2 * TOK)
                    pe.wait_ge(xt_lo_made, 2 * TOK)
                else:
                    pe.wait_ge(q_copied[1 - tile], u + tile)
                for k in range(KT):
                    mm = three(q_bank[:, :], xt_hi[:, k, cols], xt_lo[:, k, cols],
                               w_hi[wpar][:, k, 0:QW], w_lo[wpar][:, k, 0:QW], k == 0, k == KT - 1)
                mm.then_inc(q_made[tile], 1)
                if tile == 0 and not first:
                    pe.wait_ge(kv_copied[1], u)
                if tile == 1 and not first:
                    pe.wait_ge(ks_copied, u)
                if tile == 1 and first:
                    pe.wait_ge(kv_copied[0], u + 1)
                for k in range(KT):
                    mm = three(kv_bank[:, 0:2 * D], xt_hi[:, k, cols], xt_lo[:, k, cols],
                               w_hi[wpar][:, k, QW:], w_lo[wpar][:, k, QW:], k == 0, k == KT - 1)
                mm.then_inc(kv_made[tile], 1)

            def output(u, b, wo_count, between=None):
                if b == 0:
                    pe.wait_ge(wo_hi_ready, wo_count)
                    pe.wait_ge(wo_lo_ready, wo_count)
                for tile in range(TT):
                    pe.wait_ge(o_ready[tile], u + 1)
                    for h in range(GRP):
                        pe.matmul(score_bank[tile][:, :], o_r[:, tile, h, :], wo_hi[:, h, :], start=h == 0, stop=False)
                        mm = pe.matmul(score_bank[tile][:, :], o_r[:, tile, h, :], wo_lo[:, h, :], start=False,
                                       stop=h == GRP - 1)
                    mm.then_inc(out_made[tile], 1)
                    if tile == 0 and between:
                        between()

            project(0, 0, 0, 0, KT, first=True)
            project(0, 0, 1, 0, None, first=True)

            def step(g, b, first, last, odd=False, last_group=False):
                u = g * B + b
                par = int(odd)
                nb, npar = (b + 1, par) if b + 1 < B else (0, 1 - par)
                vu = v[b % 2]
                pe.wait_ge(kv_copied[0], u + 1)
                pe.wait_ge(kv_copied[1], u + 1)
                if not first:
                    pe.wait_ge(m_copied[0], u)
                for tile in range(TT):
                    t = pe.transpose(turn_bank[0][:, tile * P:(tile + 1) * P], qk[tile][:, GRP, :], ident)
                t.then_inc(kraw_turned, 1)
                pe.wait_ge(roped[0], u + 1)
                pe.wait_ge(roped[1], u + 1)
                if not first:
                    pe.wait_ge(m_copied[1], u)
                for tile in range(TT):
                    t = pe.transpose(turn_bank[1][:, tile * P:(tile + 1) * P], rc[tile][:, GRP, :], ident)
                t.then_inc(kr_turned, 1)
                for tile in range(TT):
                    pe.wait_ge((kraw_copied, kr_copied)[tile], u + 1)
                    for h in range(GRP):
                        t = pe.transpose(turn_bank[tile][:, h * P:(h + 1) * P], rc[tile][:, h, :], ident)
                    t.then_inc(qr_turned[tile], 1)
                if not last:
                    project(u + 1, nb, 0, npar, (g + 2) * KT if b == B - 1 else None)
                for half in range(2):
                    pe.wait_ge(qr_copied[half], u + 1)
                    if not (isinstance(u, int) and u < 2):
                        pe.wait_ge(out_added[half], u - 1)
                    for n in (2 * half, 2 * half + 1):
                        for hp in range(2):
                            r = (n * 2 + hp) % 4
                            q = qrT[:, n, 2 * hp:2 * hp + 2, :].rearrange("p h t -> p (h t)")
                            if n == 2:
                                pe.matmul(score_bank[1][:, r * P:r * P + W], q, krT[:, 2 * W:3 * W], start=True, stop=True)
                                mm = pe.matmul(score_bank[1][:, r * P + W:(r + 1) * P], q, krT[:, W:2 * W],
                                               start=True, stop=True)
                            else:
                                mm = pe.matmul(score_bank[half][:, r * P:(r + 1) * P], q, krT[:, half * P:(half + 1) * P],
                                               start=True, stop=True)
                    mm.then_inc(scored[half], 1)
                for tile in range(TT):
                    pe.wait_ge(es_scaled[tile], u + 1)
                    for h in range(GRP):
                        t = pe.transpose(turn_bank[tile][:, h * P:(h + 1) * P], es[tile][:, h, :], ident)
                    t.then_inc(es_turned[tile], 1)
                if not last:
                    pe.wait_ge(kv_copied[0], u + 2)
                for tile in range(TT):
                    t = pe.transpose(kv_bank[:, tile * P:(tile + 1) * P], es[tile][:, GRP, :], ident)
                t.then_inc(ks_turned, 1)
                if not last:
                    project(u + 1, nb, 1, npar, None)
                pe.wait_ge(kg_made, u + 1)
                for half in range(2):
                    pe.wait_ge(qg_made[half], u + 1)
                    if not first:
                        pe.wait_ge(o_copied[half], u)
                    for n in (2 * half, 2 * half + 1):
                        for hp in range(2):
                            r = (n * 2 + hp) % 4
                            mm = pe.matmul(lin_bank[half][:, r * P:(r + 1) * P],
                                           qg[:, n, 2 * hp:2 * hp + 2, :].rearrange("p h t -> p (h t)"),
                                           kg[:, LIN_KEYS[n], :], start=True, stop=True)
                    mm.then_inc(lin_made[half], 1)
                pe.transpose(turn_bank[0][:, 0:P], kg[:, STATE_KEYS, :], ident).then_inc(k2_turned, 1)

                def make_state():
                    pe.wait_ge(k2_copied, u + 1)
                    pe.matmul(turn_bank[1][:, 0:D], k2[:, :], vu[:, 0, :], start=True, stop=True).then_inc(state_made, 1)

                pe.wait_ge(masked[0], u + 1)
                pe.wait_ge(masked[1], u + 1)
                if first:
                    make_state()
                else:
                    pb = (b - 1) % B
                    output(u - 1, pb, g + 1 if pb == 0 else None, make_state)
                pe.wait_ge(state_copied, u + 1)
                for half in range(2):
                    pe.wait_ge(mixed[half], u + 1)
                    for r in range(4):
                        t = pe.transpose(turn_bank[half][:, r * P:(r + 1) * P], mix[:, 4 * half + r, :], ident)
                    t.then_inc(m_turned[half], 1)
                pe.wait_ge(m_copied[0], u + 1)
                pe.matmul(lin_bank[0][:, :], vu[:, 0, :], mT[:, 0:4, :], start=True, stop=True).then_inc(pv_made[0], 1)
                for n, half_cols in ((2, slice(0, 2 * P)), (3, slice(2 * P, 4 * P))):
                    pe.matmul(lin_bank[1][:, half_cols], state[:, n - 2, :],
                              qg[:, n, :, :], start=n == 2, stop=False, skip_group_check=True)
                pe.wait_ge(m_copied[1], u + 1)
                pe.wait_ge(v_mixed, u + 1)
                pe.matmul(lin_bank[1][:, 0:2 * P], vmix[:, :], mT[:, 4:6, :], start=False, stop=False, skip_group_check=True)
                pe.matmul(lin_bank[1][:, 2 * P:4 * P], vu[:, 1, :], mT[:, 6:8, :], start=False, stop=True,
                          skip_group_check=True).then_inc(pv_made[1], 1)

            over_units(pe, step)
            for tile in range(TT):
                pe.wait_ge(out_added[tile], UNITS - 1)
            output(UNITS - 1, B - 1, None)
            pe.wait_ge(fw_hi_ready, 2)
            pe.wait_ge(fw_lo_ready, 2)
            pe.wait_ge(m_copied[1], UNITS)
            for i in range(TOK + 1):
                if i < TOK:
                    turn_norm(number[(2, i)])
                if i == 1:
                    for tile in range(TT):
                        pe.wait_ge(out_added[tile], UNITS)
                if i >= 1:
                    ffn(TOK + i - 1)

        @block.scalar
        def _(act):
            def root(n):
                act.wait_ge(stats_made, 3 * n + 3)
                act.activation(dev[n % 2][:, :], meanvar[n % 2][:, 1:2], ACT.Sqrt).then_inc(dev_made, 1)

            def copy_norm(n):
                r, i = NORMS[n]
                act.wait_ge(xn_turned, n + 1)
                if r == 1:
                    act.wait_ge(ffn_made, i + 1)
                act.activation(xt_hi[:, :, i * P:(i + 1) * P], turn_bank[n % 2][:, :].rearrange("p (k t) -> p k t", k=KT),
                               ACT.Copy).then_inc(xt_hi_made, 1)

            act.wait_ge(lb_turned, 1)
            act.activation(lbT, bank[0][0:R, :], ACT.Copy).then_inc(lb_copied, 1)
            for c in range(KT):
                act.wait_ge(eff_made, c + 1)
                if c:
                    act.wait_ge(squared, c)
                act.activation(squares, eff[:, c, :], ACT.Square, accum_out=norm2[:, c:c + 1]).then_inc(squared, 1)
            act.wait_ge(squared, KT)
            act.activation(colscale[:, :], norm2[:, :], ACT.Sqrt).then_inc(rooted, 1)
            act.wait_ge(fwt_turned, KT)
            for k in range(KT):
                act.activation(fwt[:, k, :], bank[k][:, :], ACT.Copy).then_inc(fwt_copied, 1)
            act.wait_ge(fwt_copied, KT)
            act.activation(wo_hi[:, :, :], fwt[:, :, :], ACT.Copy).then_inc(fw_hi_ready, 1)
            for i in range(TOK + 2):
                if i < TOK:
                    root(number[(0, i)])
                    copy_norm(number[(0, i)])
                if 0 <= i - 2 < TOK:
                    root(number[(1, i - 2)])
                    copy_norm(number[(1, i - 2)])

            def split_chunk(g, k, par):
                act.wait_ge(w_in[k % 2], (g * 2 + (k // 2 + 1)) * 48)
                act.activation(w_hi[par][:, k, :], w_raw[k % 2][:, :], ACT.Copy).then_inc(w_hi_ready, 1)

            def split_wo(g, first=False):
                act.wait_ge(wo_in, (g + 1) * 16)
                if first:
                    act.wait_ge(ffn_made, TOK)
                else:
                    act.wait_ge(out_made[1], g * B)
                act.activation(wo_hi[:, :, :], wo_raw[:, :, :], ACT.Copy).then_inc(wo_hi_ready, 1)

            def copy_projected(u, upar, tile, first=False):
                act.wait_ge(q_made[tile], u + 1)
                if not first:
                    act.wait_ge(rotated[tile], u)
                    act.wait_ge(es_made[tile], u)
                act.activation(qk[tile][:, 0:GRP, :].rearrange("p h d -> p (h d)"), q_bank[:, :], ACT.Copy)\
                   .then_inc(q_copied[tile], 1)
                act.wait_ge(kv_made[tile], u + 1)
                if not first:
                    act.wait_ge(kraw_turned, u)
                act.activation(qk[tile][:, GRP, :], kv_bank[:, 0:D], ACT.Copy)
                if not (isinstance(u, int) and u < 2):
                    act.wait_ge(pv_made[1], u - 1)
                    act.wait_ge(v_mixed, u - 1)
                act.activation(v[upar][:, tile, :], kv_bank[:, D:2 * D], ACT.Copy).then_inc(kv_copied[tile], 1)

            def exp_projected(u, tile, first=False):
                act.wait_ge(max_made[tile], u + 1)
                act.wait_ge(q_copied[tile], u + 1)
                act.wait_ge(kv_copied[tile], u + 1)
                if not first:
                    act.wait_ge(es_turned[tile], u)
                    act.wait_ge(ks_turned, u)
                    act.wait_ge(es_recip[tile], u)
                for h in range(HEADS):
                    a = act.activation(es[tile][:, h, :], qk[tile][:, h, :], ACT.Exp, bias=nmax[tile][:, h:h + 1],
                                       accum_out=esum[tile][:, h:h + 1])
                a.then_inc(es_made[tile], 1)

            for k in range(KT):
                split_chunk(0, k, 0)
            for tile in range(TT):
                copy_projected(0, 0, tile, first=True)
                exp_projected(0, tile, first=True)

            def step(g, b, first, last, odd=False, last_group=False):
                u = g * B + b
                par = int(odd)
                act.wait_ge(kraw_turned, u + 1)
                if not first:
                    act.wait_ge(logs_made, u)
                act.activation(krawT[:, :], turn_bank[0][:, 0:N], ACT.Copy).then_inc(kraw_copied, 1)
                act.wait_ge(kr_turned, u + 1)
                if not first:
                    act.wait_ge(scored[1], u)
                act.activation(krT[:, :], turn_bank[1][:, 0:N], ACT.Copy).then_inc(kr_copied, 1)
                act.wait_ge(abs_made, u + 1)
                act.activation(lnk[:, :], lnk[:, :], ACT.Exp).then_inc(kexp_made, 1)
                for tile in range(TT):
                    act.wait_ge(qr_turned[tile], u + 1)
                    if not first:
                        act.wait_ge(scored[tile], u)
                    act.activation(qrT[:, 2 * tile:2 * tile + 2, :, :].rearrange("p n h t -> p h n t"),
                                   turn_bank[tile][:, :].rearrange("p (h n t) -> p h n t", h=GRP, n=2), ACT.Copy)\
                       .then_inc(qr_copied[tile], 1)
                    if tile == 0:
                        act.wait_ge(kexp_made, u + 1)
                        act.activation(lnk[:, :], lnk[:, :], ACT.Ln, bias=1.0).then_inc(kln_made, 1)
                if not last:
                    copy_projected(u + 1, (b + 1) % 2, 0)
                act.wait_ge(dec_bounded, u + 1)
                act.activation(dec[:, :], dec[:, :], ACT.Exp, scale=1.0 / GATE_NORM).then_inc(gates_made, 1)
                if not last:
                    exp_projected(u + 1, 0)
                act.wait_ge(ks_turned, u + 1)
                if not first:
                    act.wait_ge(kg_made, u)
                act.activation(ksT[:, :], kv_bank[:, 0:N], ACT.Copy).then_inc(ks_copied, 1)
                for half in range(2):
                    act.wait_ge(masked[half], u + 1)
                    for r in range(4 * half, 4 * half + 4):
                        a = act.activation(sc[:, r, :], sc[:, r, :], ACT.Exp, scale=-1.0, bias=scmin[:, r:r + 1],
                                           accum_out=ssum[:, r:r + 1])
                    a.then_inc(e_made[half], 1)
                if not last:
                    copy_projected(u + 1, (b + 1) % 2, 1)
                act.wait_ge(k2_turned, u + 1)
                if not first:
                    act.wait_ge(state_made, u)
                act.activation(k2[:, :], turn_bank[0][:, 0:D], ACT.Copy).then_inc(k2_copied, 1)
                if not last:
                    exp_projected(u + 1, 1)
                act.wait_ge(state_made, u + 1)
                act.wait_ge(gates_made, u + 1)
                if not first:
                    act.wait_ge(pv_made[1], u)
                act.activation(state[:, 0, :], turn_bank[1][:, 0:D], ACT.Copy)
                act.activation(state[:, 1, :], turn_bank[1][:, 0:D], ACT.Copy, scale=dec[:, DSTEP:DSTEP + 1])\
                   .then_inc(state_copied, 1)
                if not last_group:
                    for k in SPLIT_AT[b]:
                        split_chunk(g + 1, k, 1 - par)
                for half in range(2):
                    act.wait_ge(m_turned[half], u + 1)
                    if not first:
                        act.wait_ge(pv_made[half], u)
                    act.activation(mT[:, 4 * half:4 * half + 4, :].rearrange("p r q -> p (r q)"), turn_bank[half][:, :],
                                   ACT.Copy).then_inc(m_copied[half], 1)
                if b == 0:
                    split_wo(g, first=first)
                for half in range(2):
                    act.wait_ge(pv_made[half], u + 1)
                    if not first:
                        act.wait_ge(o_ready[half], u)
                    act.activation(o_bf[:, half, :, :].rearrange("p h (n t) -> p h n t", n=2),
                                   lin_bank[half][:, :].rearrange("p (n h t) -> p h n t", n=2, h=GRP),
                                   ACT.Copy, scale=0.5).then_inc(o_copied[half], 1)

            over_units(act, step)
            act.wait_ge(out_made[1], UNITS)
            act.activation(wo_hi[:, :, :], fwt[:, :, :], ACT.Copy).then_inc(fw_hi_ready, 1)
            for i in range(TOK):
                root(number[(2, i)])
                copy_norm(number[(2, i)])

        @block.vector
        def _(dve):
            def statistics(n):
                r, i = NORMS[n]
                if r == 0:
                    dve.wait_ge(x_in[i], 16)
                elif r == 1:
                    dve.wait_ge(ffn_added, i + 1)
                elif i == 0:
                    dve.wait_ge(out_added[0], UNITS)
                    dve.wait_ge(out_added[1], UNITS)
                if n >= 2:
                    dve.wait_ge(dev_made, n - 1)
                dve.bn_stats(stat[n % 2][:, :], x[:, i, :]).then_inc(stats_made, 1)
                dve.wait_ge(stats_made, 3 * n + 1)
                dve.bn_aggr(meanvar[n % 2][:, :], stat[n % 2][:, :]).then_inc(stats_made, 1)
                dve.wait_ge(stats_made, 3 * n + 2)
                dve.tensor_scalar(meanvar[n % 2][:, 1:2], meanvar[n % 2][:, 1:2], EPS, None, ALU.add)\
                   .then_inc(stats_made, 1)

            def normalise(n):
                r, i = NORMS[n]
                dve.wait_ge(dev_made, n + 1)
                dve.reciprocal(rstd[n % 2][:, :], dev[n % 2][:, :]).then_inc(rstd_made, 1)
                dve.wait_ge(rstd_made, n + 1)
                if n >= 2:
                    dve.wait_ge(xn_turned, n - 1)
                dve.tensor_scalar(xn[n % 2], x[:, i, :], meanvar[n % 2][:, 0:1], rstd[n % 2][:, 0:1],
                                  ALU.subtract, ALU.mult).then_inc(xn_made, 1)

            def rest_norm(n):
                r, i = NORMS[n]
                cols = slice(i * P, (i + 1) * P)
                dve.wait_ge(xt_hi_made, n + 1)
                dve.tensor_tensor(xt_lo[:, :, cols], turn_bank[n % 2][:, :].rearrange("p (k t) -> p k t", k=KT),
                                  xt_hi[:, :, cols].bitcast(F32), ALU.subtract).then_inc(xt_lo_made, 1)

            def add_ffn(f):
                dve.wait_ge(ffn_made, f + 1)
                dve.tensor_tensor(x[:, f % TOK, :], score_bank[f % 2][:, :], x[:, f % TOK, :], ALU.add)\
                   .then_inc(ffn_added, 1)

            dve.wait_ge(fw_in, 32)
            for c in range(KT):
                dve.wait_ge(ba_made, c + 1)
                dve.tensor_tensor(eff[:, c, :], bank[4 + c][:, :], fwt[:, c, :], ALU.add).then_inc(eff_made, 1)
            dve.wait_ge(rooted, 1)
            dve.reciprocal(norm2[:, :], colscale[:, :]).then_inc(scaled_c, 1)
            dve.wait_ge(scaled_c, 1)
            dve.scalar_tensor_tensor(out=colscale[:, :], in0=norm2[:, :], scalar=0.5, in1=magc[:, :],
                                     op0=ALU.mult, op1=ALU.mult).then_inc(scaled_c, 1)
            dve.wait_ge(scaled_c, 2)
            for c in range(KT):
                dve.tensor_scalar(eff[:, c, :], eff[:, c, :], colscale[:, c:c + 1], None, ALU.mult).then_inc(eff_scaled, 1)
            dve.wait_ge(fw_hi_ready, 1)
            dve.tensor_tensor(wo_lo[:, :, :], fwt[:, :, :], wo_hi[:, :, :].bitcast(F32), ALU.subtract)\
               .then_inc(fw_lo_ready, 1)
            for i in range(TOK + 3):
                if i < TOK:
                    n = number[(0, i)]
                    statistics(n)
                    normalise(n)
                if 0 <= i - 2 < TOK:
                    n = number[(1, i - 2)]
                    add_ffn(i - 2)
                    statistics(n)
                    normalise(n)
                if i < TOK:
                    rest_norm(number[(0, i)])
                if 0 <= i - 2 < TOK:
                    rest_norm(number[(1, i - 2)])

            def prepare(u, tile, first=False):
                dve.wait_ge(q_copied[tile], u + 1)
                dve.wait_ge(kv_copied[tile], u + 1)
                if not first:
                    dve.wait_ge(es_made[tile], u)
                dve.tensor_reduce(nmax[tile][:, :], qk[tile][:, :, :], AX_X, ALU.max, negate=True)\
                   .then_inc(max_made[tile], 1)
                if not first:
                    dve.wait_ge(roped[tile], u)
                    dve.wait_ge(kr_turned, u)
                    dve.wait_ge(qr_turned[tile], u)
                dve.tensor_tensor(rc[tile][:, :, :], qk[tile][:, :, :],
                                  cos[:, tile, :].unsqueeze(1).to_broadcast([P, HEADS, D]), ALU.mult)
                for a, b in ((0, D // 2), (D // 2, 0)):
                    r = dve.tensor_tensor(rs[tile][:, :, a:a + D // 2], qk[tile][:, :, b:b + D // 2],
                                          sin[:, tile, a:a + D // 2].unsqueeze(1).to_broadcast([P, HEADS, D // 2]),
                                          ALU.mult)
                r.then_inc(rotated[tile], 1)

            def invert(u, tile, first=False):
                dve.wait_ge(es_made[tile], u + 1)
                if not first:
                    dve.wait_ge(es_scaled[tile], u)
                dve.reciprocal(erec[tile][:, :], esum[tile][:, :]).then_inc(es_recip[tile], 1)

            def add_output(u, b):
                for tile in range(TT):
                    i = b * TT + tile
                    dve.wait_ge(out_made[tile], u + 1)
                    dve.tensor_tensor(x[:, i, :], score_bank[tile][:, :], x[:, i, :], ALU.add).then_inc(out_added[tile], 1)

            for tile in range(TT):
                prepare(0, tile, first=True)
                invert(0, tile, first=True)

            def step(g, b, first, last, odd=False, last_group=False):
                u = g * B + b
                dve.wait_ge(kraw_copied, u + 1)
                dve.scalar_tensor_tensor(out=lnk[:, :], in0=krawT[:, :], scalar=-1.0, in1=krawT[:, :],
                                         op0=ALU.mult, op1=ALU.min).then_inc(abs_made, 1)
                dve.wait_ge(kv_copied[0], u + 1)
                dve.wait_ge(kv_copied[1], u + 1)
                if not first:
                    dve.wait_ge(pv_made[1], u)
                dve.tensor_copy(vmix[0:W, :], v[b % 2][0:W, 1, :])
                dve.tensor_copy(vmix[W:P, :], v[b % 2][W:P, 0, :]).then_inc(v_mixed, 1)
                dve.wait_ge(kln_made, u + 1)
                dve.scalar_tensor_tensor(out=logs[:, :], in0=krawT[:, :], scalar=0.0, in1=lnk[:, :],
                                         op0=ALU.min, op1=ALU.subtract).then_inc(logs_made, 1)
                dve.wait_ge(logs_made, u + 1)
                dve.tensor_tensor_scan(G[:, :], ones, logs[:, :], 0.0, ALU.mult, ALU.add).then_inc(summed, 1)
                dve.wait_ge(summed, u + 1)
                if not first:
                    dve.wait_ge(state_copied, u)
                mid = G[:, W // 2 - 1::W]
                dve.tensor_tensor(dec[:, 0:3 * P].rearrange("p (n s) -> p n s", n=3),
                                  mid[:, 0:3].unsqueeze(2).to_broadcast([P, 3, P]),
                                  G[:, 0:P].unsqueeze(1).to_broadcast([P, 3, P]), ALU.subtract)
                dve.tensor_tensor(dec[:, 3 * P:5 * P].rearrange("p (n s) -> p n s", n=2),
                                  mid[:, 2:4].unsqueeze(2).to_broadcast([P, 2, P]),
                                  G[:, P:2 * P].unsqueeze(1).to_broadcast([P, 2, P]), ALU.subtract)
                dve.tensor_tensor(dec[:, DQ:DSTEP].rearrange("p (n s) -> p n s", n=NB),
                                  G[:, :].rearrange("p (n s) -> p n s", n=NB),
                                  mid.unsqueeze(2).to_broadcast([P, NB, W]), ALU.subtract)
                dve.tensor_tensor(dec[:, DSTEP:DSTEP + 1], mid[:, 3:4], mid[:, 2:3], ALU.subtract).then_inc(dec_made, 1)
                dve.wait_ge(dec_made, u + 1)
                dve.tensor_scalar(dec[:, :], dec[:, :], MOST, None, ALU.min).then_inc(dec_bounded, 1)
                if not last:
                    prepare(u + 1, 0)
                for half in range(2):
                    dve.wait_ge(scored[half], u + 1)
                    dve.nop(nofuse=True)
                    for r in range(4 * half, 4 * half + 4):
                        m = dve.tensor_tensor_reduce(sc[:, r, :], score_bank[half][:, (r % 4) * P:(r % 4 + 1) * P],
                                                     win[:, WIN_OF_BLOCK[r // 2], :], -float(D) ** -0.5, BIG,
                                                     ALU.add, ALU.min, scmin[:, r:r + 1])
                    m.then_inc(masked[half], 1)
                if not last:
                    invert(u + 1, 0)
                dve.wait_ge(gates_made, u + 1)
                for tile in range(TT):
                    dve.wait_ge(es_turned[tile], u + 1)
                    if not first:
                        dve.wait_ge(lin_made[tile], u)
                        dve.wait_ge(pv_made[1], u)
                    dve.tensor_tensor(qg[:, 2 * tile:2 * tile + 2, :, :].rearrange("p n h t -> p h n t"),
                                      turn_bank[tile][:, :].rearrange("p (h n t) -> p h n t", h=GRP, n=2),
                                      dec[:, DQ + tile * P:DQ + (tile + 1) * P].rearrange("p (n t) -> p n t", n=2)
                                      .unsqueeze(1).to_broadcast([P, GRP, 2, W]),
                                      ALU.mult).then_inc(qg_made[tile], 1)
                dve.wait_ge(ks_copied, u + 1)
                if not first:
                    dve.wait_ge(lin_made[1], u)
                    dve.wait_ge(k2_turned, u)
                dve.tensor_tensor(kg[:, 0:3, :], ksT[:, 0:P].unsqueeze(1).to_broadcast([P, 3, P]),
                                  dec[:, 0:3 * P].rearrange("p (n s) -> p n s", n=3), ALU.mult)
                dve.tensor_tensor(kg[:, 3:5, :], ksT[:, P:2 * P].unsqueeze(1).to_broadcast([P, 2, P]),
                                  dec[:, 3 * P:5 * P].rearrange("p (n s) -> p n s", n=2), ALU.mult).then_inc(kg_made, 1)
                if not last:
                    prepare(u + 1, 1)
                for half in range(2):
                    rows = slice(4 * half, 4 * half + 4)
                    dve.wait_ge(e_made[half], u + 1)
                    dve.reciprocal(srec[:, rows], ssum[:, rows]).then_inc(e_recip[half], 1)
                    dve.wait_ge(lin_made[half], u + 1)
                    if not first:
                        dve.wait_ge(m_turned[half], u)
                    dve.tensor_tensor(mix[:, rows, :].rearrange("p (n h) k -> p n h k", n=2),
                                      lin_bank[half][:, :].rearrange("p (n h k) -> p n h k", n=2, h=2),
                                      lin.unsqueeze(2).to_broadcast([P, 2, 2, P]), ALU.min).then_inc(lin_masked[half], 1)
                    dve.wait_ge(e_recip[half], u + 1)
                    dve.wait_ge(lin_masked[half], u + 1)
                    for r in range(4 * half, 4 * half + 4):
                        m = dve.scalar_tensor_tensor(out=mix[:, r, :], in0=sc[:, r, :], scalar=srec[:, r:r + 1],
                                                     in1=mix[:, r, :], op0=ALU.mult, op1=ALU.add)
                    m.then_inc(mixed[half], 1)
                if not last:
                    invert(u + 1, 1)
                if not first:
                    add_output(u - 1, (b - 1) % B)

            over_units(dve, step)
            add_output(UNITS - 1, B - 1)
            dve.wait_ge(fw_hi_ready, 2)
            dve.tensor_tensor(wo_lo[:, :, :], fwt[:, :, :], wo_hi[:, :, :].bitcast(F32), ALU.subtract)\
               .then_inc(fw_lo_ready, 1)
            for i in range(TOK + 2):
                if i < TOK:
                    n = number[(2, i)]
                    statistics(n)
                    normalise(n)
                    rest_norm(n)
                if i >= 2:
                    add_ffn(TOK + i - 2)

        @block.gpsimd
        def _(pool):
            def split_chunk(g, k, par):
                pool.wait_ge(w_hi_ready, g * KT + (k + 1))
                pool.tensor_tensor(w_lo[par][:, k, :], w_raw[k % 2][:, :], w_hi[par][:, k, :].bitcast(F32), ALU.subtract)\
                    .then_inc(w_lo_ready, 1)

            def split_wo(g):
                pool.wait_ge(wo_hi_ready, g + 1)
                pool.tensor_tensor(wo_lo[:, :, :], wo_raw[:, :, :], wo_hi[:, :, :].bitcast(F32), ALU.subtract)\
                    .then_inc(wo_lo_ready, 1)

            def rope(u, tile):
                pool.wait_ge(rotated[tile], u + 1)
                pool.tensor_tensor(rc[tile][:, :, :], rc[tile][:, :, :], rs[tile][:, :, :], ALU.add)\
                    .then_inc(roped[tile], 1)

            def scale(u, tile):
                pool.wait_ge(es_recip[tile], u + 1)
                pool.tensor_tensor(es[tile][:, :, :], es[tile][:, :, :],
                                   erec[tile][:, :].unsqueeze(2).to_broadcast([P, HEADS, D]), ALU.mult)\
                    .then_inc(es_scaled[tile], 1)

            for k in range(KT):
                split_chunk(0, k, 0)
            for tile in range(TT):
                rope(0, tile)
                scale(0, tile)

            def step(g, b, first, last, odd=False, last_group=False):
                u = g * B + b
                par = int(odd)
                if not last:
                    rope(u + 1, 0)
                    scale(u + 1, 0)
                    rope(u + 1, 1)
                    scale(u + 1, 1)
                if not last_group:
                    for k in SPLIT_AT[b]:
                        split_chunk(g + 1, k, 1 - par)
                if b == 0:
                    split_wo(g)
                for half in range(2):
                    pool.wait_ge(o_copied[half], u + 1)
                    if not first:
                        pool.wait_ge(out_made[half], u)
                    pool.nop(nofuse=True)
                    pool.tensor_copy(o_r[:, half, :, :], o_bf[:, half, :, :]).then_inc(o_ready[half], 1)

            over_units(pool, step)


def shape_constants():
    import numpy as np
    c = np.zeros((P, C_ALL), np.float32)
    half = np.arange(D // 2, dtype=np.float32)
    inv = np.float32(1.0) / np.power(np.float32(10000.0), np.float32(2.0) * half / np.float32(D))
    fr = np.arange(N, dtype=np.float32)[:, None] * inv[None, :].astype(np.float32)
    cos, sin = np.cos(fr), np.sin(fr)
    for t in range(TT):
        rows = slice(t * P, (t + 1) * P)
        c[:, C_COS + t * D:C_COS + (t + 1) * D] = np.concatenate([cos[rows], cos[rows]], 1)
        c[:, C_SIN + t * D:C_SIN + (t + 1) * D] = np.concatenate([-sin[rows], sin[rows]], 1)
    t = np.arange(P)[:, None] % W
    k = np.arange(P)[None, :]
    own, back = k % W <= t, k % W >= t
    early = k < W
    windows = (early & own, (early & back) | (~early & own), (early & own) | (~early & back))
    for i, seen in enumerate(windows):
        c[:, C_WIN + i * P:C_WIN + (i + 1) * P] = np.where(seen, 0.0, FAR)
    for i, seen in enumerate((early & own, early | own)):
        c[:, C_LIN + i * P:C_LIN + (i + 1) * P] = np.where(seen, BIG, 0.0)
    c[:, C_ID:C_ONE] = np.eye(P)
    c[:, C_ONE:] = 1.0
    return c


def kernel(L0_attn_hidden_states, L0_attn_Wq, L0_attn_Wk, L0_attn_Wv, L0_attn_Wo, L0_ffn_W, L0_ffn_lora_A,
           L0_ffn_lora_B, L0_ffn_magnitude):
    import numpy as np
    import concourse.bacc as bacc
    from concourse.bass_utils import run_bass_kernel_spmd

    nc = bacc.Bacc("TRN2", target_bir_lowering=False, num_devices=1)
    arrays = {
        "hs": np.ascontiguousarray(L0_attn_hidden_states).reshape(B * N, HID),
        "wq": L0_attn_Wq, "wk": L0_attn_Wk, "wv": L0_attn_Wv, "wo": L0_attn_Wo,
        "fw": L0_ffn_W, "la": L0_ffn_lora_A, "lb": L0_ffn_lora_B,
        "mag": np.asarray(L0_ffn_magnitude).reshape(KT, P).T,
        "consts": shape_constants(),
    }
    arrays = {f"{name}_dram": np.ascontiguousarray(a) for name, a in arrays.items()}
    args = [nc.dram_tensor(name, a.shape, mybir.dt.from_np(a.dtype), kind="ExternalInput").ap()
            for name, a in arrays.items()]
    args.append(nc.dram_tensor("out_dram", (B * N, HID), F32, kind="ExternalOutput").ap())
    layer_program(nc, *args)
    r = run_bass_kernel_spmd(nc, [arrays], core_ids=[0])
    return r.results[0]["out_dram"].reshape(B, N, HID)
```

```python
from contextlib import ExitStack

import concourse.bass as bass
from concourse import mybir

P = 128
B, N, HID = 4, 256, 512
H, KVH, D, W = 32, 8, 128, 64
R = 32
GRP = H // KVH
HEADS = GRP + 1
KT = HID // P
TOK = B * N // P
TT = N // P
NB = N // W
QW = GRP * D
UNITS = KVH * B
EPS = 1e-5
GATE_NORM = 16.0
MOST = 85.0 * GATE_NORM
FAR = -1.0e30
BIG = 3.0e38

F32 = mybir.dt.float32
F32R = mybir.dt.float32r
BF16 = mybir.dt.bfloat16
ALU = mybir.AluOpType
ACT = mybir.ActivationFunctionType
AX_X = mybir.AxisListType.X

KEYS = 5
DQ = KEYS * P
DSTEP = DQ + N
LIN_KEYS = (0, 1, 3, 4)
STATE_KEYS = 2

C_COS, C_SIN, C_WIN, C_LIN, C_ID, C_ONE = 0, TT * D, 2 * TT * D, 2 * TT * D + 3 * P, 2 * TT * D + 5 * P, 2 * TT * D + 6 * P
C_ALL = C_ONE + N
SPLIT_AT = ((0,), (1,), (2, 3), ())
WIN_OF_BLOCK = (0, 1, 2, 1)


def layer_program(nc, hs, wq, wk, wv, wo, fw, la, lb, mag, consts, out):
    ctx = ExitStack()
    with ctx:
        def sb(name, shape, dt=F32):
            return ctx.enter_context(nc.sbuf_tensor(name, shape, dt))

        def sem(name):
            return ctx.enter_context(nc.semaphore(name))

        def sems(name, n=2):
            return [sem(f"{name}{i}") for i in range(n)]

        x = sb("x", [P, TOK, HID])
        xt_hi = sb("xt_hi", [P, KT, TOK * P], F32R)
        xt_lo = sb("xt_lo", [P, KT, TOK * P], F32R)
        w_hi = [sb(f"w_hi{i}", [P, KT, QW + 2 * D], F32R) for i in range(2)]
        w_lo = [sb(f"w_lo{i}", [P, KT, QW + 2 * D], F32R) for i in range(2)]
        w_raw = [sb(f"w_raw{i}", [P, QW + 2 * D]) for i in range(2)]
        wo_hi = sb("wo_hi", [P, GRP, HID], F32R)
        wo_lo = sb("wo_lo", [P, GRP, HID], F32R)
        wo_raw = sb("wo_raw", [P, GRP, HID])
        fwt = sb("fwt", [P, KT, HID])
        cst = sb("cst", [P, C_ALL])
        qk = [sb(f"qk{i}", [P, HEADS, D]) for i in range(TT)]
        rc = [sb(f"rc{i}", [P, HEADS, D]) for i in range(TT)]
        rs = [sb(f"rs{i}", [P, HEADS, D]) for i in range(TT)]
        es = [sb(f"es{i}", [P, HEADS, D]) for i in range(TT)]
        v = [sb(f"v{i}", [P, TT, D]) for i in range(2)]
        vmix = sb("vmix", [P, D])
        krawT = sb("krawT", [P, N])
        krT = sb("krT", [P, N])
        ksT = sb("ksT", [P, N])
        lnk = sb("lnk", [P, N])
        logs = sb("logs", [P, N])
        G = sb("G", [P, N])
        dec = sb("dec", [P, DSTEP + 1])
        kg = sb("kg", [P, KEYS, P])
        qrT = sb("qrT", [P, NB, GRP, W])
        qg = sb("qg", [P, NB, GRP, W])
        k2 = sb("k2", [P, D])
        state = sb("state", [P, 2, D])
        sc = sb("sc", [P, 8, P])
        mix = sb("mix", [P, 8, P])
        mT = sb("mT", [P, 8, P])
        o_bf = sb("o_bf", [P, TT, GRP, P], BF16)
        o_r = sb("o_r", [P, TT, GRP, P], F32R)
        nmax = [sb(f"nmax{i}", [P, HEADS]) for i in range(TT)]
        esum = [sb(f"esum{i}", [P, HEADS]) for i in range(TT)]
        erec = [sb(f"erec{i}", [P, HEADS]) for i in range(TT)]
        scmin = sb("scmin", [P, 8])
        ssum = sb("ssum", [P, 8])
        srec = sb("srec", [P, 8])
        stat = sb("stat", [P, TOK, 6])
        meanvar = sb("meanvar", [P, TOK, 2])
        dev = sb("dev", [P, TOK])
        rstd = sb("rstd", [P, TOK])
        magc = sb("magc", [P, KT])
        norm2 = sb("norm2", [P, KT])
        colscale = sb("colscale", [P, KT])
        first_half, second_half = slice(0, 4), slice(4, 8)
        xn = [[t[:, hf, :].rearrange("p a b -> p (a b)") for hf in (first_half, second_half)] for t in (sc, mix)]
        squares = [qk[i][:, 0:GRP, :].rearrange("p a b -> p (a b)") for i in range(TT)]
        eff = wo_raw
        ff_hi = [w_hi[i][:, :, 0:HID] for i in (1, 0)]
        ff_lo = [w_lo[i][:, :, 0:HID] for i in (1, 0)]
        lbT = mT[0:R, 0:4, :].rearrange("p a b -> p (a b)")
        la_sb = mT[0:R, 4:8, :].rearrange("p a b -> p (a b)")
        lb_sb = k2[:, :].rearrange("p (c r) -> p c r", r=R)

        cos = cst[:, C_COS:C_SIN].rearrange("p (t d) -> p t d", d=D)
        sin = cst[:, C_SIN:C_WIN].rearrange("p (t d) -> p t d", d=D)
        win = cst[:, C_WIN:C_LIN].rearrange("p (n k) -> p n k", k=P)
        lin = cst[:, C_LIN:C_ID].rearrange("p (n k) -> p n k", k=P)
        ident = cst[:, C_ID:C_ONE]
        ones = cst[:, C_ONE:C_ALL]

        bank = [ctx.enter_context(nc.psum_tensor(f"bank{i}", [P, 512], F32)) for i in range(8)]
        q_bank, kv_bank = bank[0], bank[1]
        norm_bank = (bank[6:8], bank[2:4], bank[2:4])
        turn_bank = bank[2:4]
        score_bank = bank[4:6]
        lin_bank = bank[6:8]

        x_in = sems("x_in", TOK)
        cst_in, fw_in, lora_in = sem("cst_in"), sem("fw_in"), sem("lora_in")
        lb_turned, lb_copied, ba_made, eff_made = sem("lb_turned"), sem("lb_copied"), sem("ba_made"), sem("eff_made")
        squared, rooted, scaled_c, eff_scaled = sem("squared"), sem("rooted"), sem("scaled_c"), sem("eff_scaled")
        fwt_turned, fwt_copied = sem("fwt_turned"), sem("fwt_copied")
        fw_hi_ready, fw_lo_ready = sem("fw_hi_ready"), sem("fw_lo_ready")
        stats_made, aggregated, eps_added = sems("stats_made", 3), sems("aggregated", 3), sems("eps_added", 3)
        dev_made, rstd_made, xn_made = sems("dev_made", 3), sems("rstd_made", 3), sems("xn_made", 3)
        xn_turned, xt_hi_made, xt_lo_made = sems("xn_turned", 3), sems("xt_hi_made", 3), sems("xt_lo_made", 3)
        ffn_made, ffn_added, stored = sem("ffn_made"), sem("ffn_added"), sem("stored")

        w_in = sems("w_in")
        wo_in = sem("wo_in")
        w_hi_ready, w_lo_ready = sem("w_hi_ready"), sem("w_lo_ready")
        wo_hi_ready, wo_lo_ready = sem("wo_hi_ready"), sem("wo_lo_ready")

        q_made, kv_made = sems("q_made"), sems("kv_made")
        q_copied, kv_copied = sems("q_copied"), sems("kv_copied")
        max_made, rotated, roped = sems("max_made"), sems("rotated"), sems("roped")
        es_made, es_recip, es_scaled = sems("es_made"), sems("es_recip"), sems("es_scaled")
        v_mixed = sem("v_mixed")
        kraw_turned, kr_turned, ks_turned = sem("kraw_turned"), sem("kr_turned"), sem("ks_turned")
        kraw_copied, kr_copied, ks_copied = sem("kraw_copied"), sem("kr_copied"), sem("ks_copied")
        qr_turned, qr_copied, es_turned = sems("qr_turned"), sems("qr_copied"), sems("es_turned")
        abs_made, kexp_made, kln_made = sem("abs_made"), sem("kexp_made"), sem("kln_made")
        logs_made, summed, dec_made, dec_bounded, gates_made = (
            sem("logs_made"), sem("summed"), sem("dec_made"), sem("dec_bounded"), sem("gates_made"))
        kg_made, qg_made = sem("kg_made"), sems("qg_made")
        k2_turned, k2_copied, state_made, state_copied = (
            sem("k2_turned"), sem("k2_copied"), sem("state_made"), sem("state_copied"))
        scored, masked, e_made, e_recip = sems("scored"), sems("masked"), sems("e_made"), sems("e_recip")
        lin_made, lin_masked, mixed = sems("lin_made"), sems("lin_masked"), sems("mixed")
        m_turned, m_copied, pv_made, o_copied, o_ready = (
            sems("m_turned"), sems("m_copied"), sems("pv_made"), sems("o_copied"), sems("o_ready"))
        out_made, out_added = sems("out_made"), sems("out_added")

        def over_units(eng, step):
            for b in range(B):
                step(0, b, first=b == 0, last=False)
            with eng.Fori(1, KVH - 1, 2) as g:
                for b in range(B):
                    step(g, b, first=False, last=False, odd=True)
                for b in range(B):
                    step(g + 1, b, first=False, last=False)
            for b in range(B):
                step(KVH - 1, b, first=False, last=b == B - 1, odd=True, last_group=True)

        block = ctx.enter_context(nc.Block())

        @block.sync
        def _(sp):
            sp.dma_start(cst[:, :], consts).then_inc(cst_in, 16)
            sp.dma_start(lb_sb, lb.rearrange("(c p) r -> p c r", p=P)).then_inc(lora_in, 16)
            sp.dma_start(la_sb, la).then_inc(lora_in, 16)
            sp.dma_start(fwt[:, :, :], fw.rearrange("(c p) i -> p c i", p=P)).then_inc(fw_in, 16)
            sp.dma_start(magc[:, :], mag).then_inc(fw_in, 16)
            for i in range(TOK):
                sp.dma_start(x[:, i, :], hs[i * P:(i + 1) * P, :]).then_inc(x_in[i], 16)

            def load_chunk(g, k):
                s = k % 2
                rows = slice(k * P, (k + 1) * P)
                sp.dma_start(w_raw[s][:, 0:QW], wq[rows, bass.ds(g * QW, QW)]).then_inc(w_in[s], 16)
                sp.dma_start(w_raw[s][:, QW:QW + D], wk[rows, bass.ds(g * D, D)]).then_inc(w_in[s], 16)
                sp.dma_start(w_raw[s][:, QW + D:], wv[rows, bass.ds(g * D, D)]).then_inc(w_in[s], 16)

            for k in range(KT):
                if k >= 2:
                    sp.wait_ge(w_hi_ready, k - 1)
                    sp.wait_ge(w_lo_ready, k - 1)
                load_chunk(0, k)
            sp.wait_ge(fwt_turned, KT)
            sp.dma_start(wo_raw[:, :, :], wo[0:QW, :].rearrange("(h d) n -> d h n", d=D)).then_inc(wo_in, 16)
            with sp.Fori(1, KVH) as g:
                for k in range(KT):
                    sp.wait_ge(w_hi_ready, g * KT + (k - 1))
                    sp.wait_ge(w_lo_ready, g * KT + (k - 1))
                    load_chunk(g, k)
                    if k == KT - 1:
                        sp.wait_ge(wo_hi_ready, g * GRP)
                        sp.wait_ge(wo_lo_ready, g * GRP)
                        sp.dma_start(wo_raw[:, :, :], wo[bass.ds(g * QW, QW), :].rearrange("(h d) n -> d h n", d=D))\
                          .then_inc(wo_in, 16)
            for i in range(TOK):
                sp.wait_ge(ffn_added, TOK + i + 1)
                sp.dma_start(out[i * P:(i + 1) * P, :], x[:, i, :]).then_inc(stored, 16)
            sp.wait_ge(stored, 16 * TOK)

        @block.tensor
        def _(pe):
            def three(dst, a_hi, a_lo, b_hi, b_lo, start, stop):
                pe.matmul(dst, a_hi, b_hi, start=start, stop=False)
                pe.matmul(dst, a_hi, b_lo, start=False, stop=False)
                return pe.matmul(dst, a_lo, b_hi, start=False, stop=stop)

            def turn_norm(r, i):
                pe.wait_ge(xn_made[r], i + 1)
                if i >= 2:
                    pe.wait_ge(xt_lo_made[r], i - 1)
                for k in range(KT):
                    t = pe.transpose(norm_bank[r][i % 2][:, k * P:(k + 1) * P], xn[r % 2][i % 2][:, k * P:(k + 1) * P],
                                     ident)
                t.then_inc(xn_turned[r], 1)

            def ffn(f):
                i, second = f % TOK, f // TOK
                pe.wait_ge(xt_hi_made[2 * second], i + 1)
                pe.wait_ge(xt_lo_made[2 * second], i + 1)
                if i >= 2:
                    pe.wait_ge(ffn_added, f - 1)
                for k in range(KT):
                    if i == 0:
                        pe.wait_ge(fw_hi_ready, second * KT + k + 1)
                        pe.wait_ge(fw_lo_ready, second * KT + k + 1)
                    cols = slice(i * P, (i + 1) * P)
                    mm = three(score_bank[f % 2][:, :], xt_hi[:, k, cols], xt_lo[:, k, cols],
                               ff_hi[second][:, k, :], ff_lo[second][:, k, :], k == 0, k == KT - 1)
                mm.then_inc(ffn_made, 1)

            pe.wait_ge(cst_in, 16)
            pe.wait_ge(lora_in, 32)
            for c in range(KT):
                t = pe.transpose(bank[0][0:R, c * P:(c + 1) * P], lb_sb[:, c, :], ident)
            t.then_inc(lb_turned, 1)
            pe.wait_ge(lb_copied, 1)
            for c in range(KT):
                pe.matmul(bank[4 + c][:, :], lbT[:, c * P:(c + 1) * P], la_sb, start=True, stop=True).then_inc(ba_made, 1)
            for c in range(KT):
                pe.wait_ge(eff_scaled, c + 1)
                for k in range(KT):
                    t = pe.transpose(bank[k][:, c * P:(c + 1) * P], eff[:, c, k * P:(k + 1) * P], ident)
                t.then_inc(fwt_turned, 1)
            for i in range(TOK + 2):
                if i < TOK:
                    turn_norm(0, i)
                if i == 3:
                    pe.wait_ge(fwt_copied, KT)
                if 0 <= i - 1 < TOK:
                    ffn(i - 1)
                if 0 <= i - 4 < TOK - TT:
                    turn_norm(1, i - 4)

            def project(u, b, tile, wpar, new_weights, first=False):
                if new_weights is not None:
                    pe.wait_ge(w_hi_ready, new_weights)
                    pe.wait_ge(w_lo_ready, new_weights)
                i = b * TT + tile
                cols = slice(i * P, (i + 1) * P)
                if first:
                    pe.wait_ge(xt_hi_made[1], tile + 1)
                    pe.wait_ge(xt_lo_made[1], tile + 1)
                if first and tile == 0:
                    pass
                elif tile == 0:
                    pe.wait_ge(kraw_copied, u)
                else:
                    pe.wait_ge(q_copied[0], u + 1)
                for k in range(KT):
                    mm = three(q_bank[:, :], xt_hi[:, k, cols], xt_lo[:, k, cols],
                               w_hi[wpar][:, k, 0:QW], w_lo[wpar][:, k, 0:QW], k == 0, k == KT - 1)
                mm.then_inc(q_made[tile], 1)
                if tile == 0 and not first:
                    pe.wait_ge(kr_copied, u)
                if tile == 1 and not first:
                    pe.wait_ge(ks_copied, u)
                if tile == 1 and first:
                    pe.wait_ge(kv_copied[0], u + 1)
                for k in range(KT):
                    mm = three(kv_bank[:, 0:2 * D], xt_hi[:, k, cols], xt_lo[:, k, cols],
                               w_hi[wpar][:, k, QW:], w_lo[wpar][:, k, QW:], k == 0, k == KT - 1)
                mm.then_inc(kv_made[tile], 1)

            def output(u, b, wo_count, between=None):
                if b == 0:
                    pe.wait_ge(wo_hi_ready, wo_count)
                    pe.wait_ge(wo_lo_ready, wo_count)
                for tile in range(TT):
                    pe.wait_ge(o_ready[tile], u + 1)
                    for h in range(GRP):
                        pe.matmul(score_bank[tile][:, :], o_r[:, tile, h, :], wo_hi[:, h, :], start=h == 0, stop=False)
                        mm = pe.matmul(score_bank[tile][:, :], o_r[:, tile, h, :], wo_lo[:, h, :], start=False,
                                       stop=h == GRP - 1)
                    mm.then_inc(out_made[tile], 1)
                    if tile == 0 and between:
                        between()

            for tile in range(TT):
                project(0, 0, tile, 0, KT if tile == 0 else None, first=True)
                turn_norm(1, TOK - TT + tile)
            for i in range(TT, TOK):
                pe.wait_ge(xt_hi_made[1], i + 1)
                pe.wait_ge(xt_lo_made[1], i + 1)

            def step(g, b, first, last, odd=False, last_group=False):
                u = g * B + b
                par = int(odd)
                nb, npar = (b + 1, par) if b + 1 < B else (0, 1 - par)
                vu = v[b % 2]
                pe.wait_ge(kv_copied[0], u + 1)
                pe.wait_ge(kv_copied[1], u + 1)
                for tile in range(TT):
                    t = pe.transpose(q_bank[:, tile * P:(tile + 1) * P], qk[tile][:, GRP, :], ident)
                t.then_inc(kraw_turned, 1)
                pe.wait_ge(roped[0], u + 1)
                pe.wait_ge(roped[1], u + 1)
                for tile in range(TT):
                    t = pe.transpose(kv_bank[:, tile * P:(tile + 1) * P], rc[tile][:, GRP, :], ident)
                t.then_inc(kr_turned, 1)
                for tile in range(TT):
                    if not first:
                        pe.wait_ge(m_copied[tile], u)
                    for h in range(GRP):
                        t = pe.transpose(turn_bank[tile][:, h * P:(h + 1) * P], rc[tile][:, h, :], ident)
                    t.then_inc(qr_turned[tile], 1)
                if not last:
                    project(u + 1, nb, 0, npar, (g + 2) * KT if b == B - 1 else None)
                for half in range(2):
                    pe.wait_ge(qr_copied[half], u + 1)
                    if not (isinstance(u, int) and u < 2):
                        pe.wait_ge(out_added[half], u - 1)
                    for n in (2 * half, 2 * half + 1):
                        for hp in range(2):
                            r = (n * 2 + hp) % 4
                            q = qrT[:, n, 2 * hp:2 * hp + 2, :].rearrange("p h t -> p (h t)")
                            if n == 2:
                                pe.matmul(score_bank[1][:, r * P:r * P + W], q, krT[:, 2 * W:3 * W], start=True, stop=True)
                                mm = pe.matmul(score_bank[1][:, r * P + W:(r + 1) * P], q, krT[:, W:2 * W],
                                               start=True, stop=True)
                            else:
                                mm = pe.matmul(score_bank[half][:, r * P:(r + 1) * P], q, krT[:, half * P:(half + 1) * P],
                                               start=True, stop=True)
                    mm.then_inc(scored[half], 1)
                for tile in range(TT):
                    pe.wait_ge(es_scaled[tile], u + 1)
                    for h in range(GRP):
                        t = pe.transpose(turn_bank[tile][:, h * P:(h + 1) * P], es[tile][:, h, :], ident)
                    t.then_inc(es_turned[tile], 1)
                if last:
                    pe.wait_ge(kr_copied, u + 1)
                else:
                    pe.wait_ge(kv_copied[0], u + 2)
                for tile in range(TT):
                    t = pe.transpose(kv_bank[:, tile * P:(tile + 1) * P], es[tile][:, GRP, :], ident)
                t.then_inc(ks_turned, 1)
                if not last:
                    project(u + 1, nb, 1, npar, None)
                pe.wait_ge(kg_made, u + 1)
                for half in range(2):
                    pe.wait_ge(qg_made[half], u + 1)
                    if not first:
                        pe.wait_ge(o_copied[half], u)
                    for n in (2 * half, 2 * half + 1):
                        for hp in range(2):
                            r = (n * 2 + hp) % 4
                            mm = pe.matmul(lin_bank[half][:, r * P:(r + 1) * P],
                                           qg[:, n, 2 * hp:2 * hp + 2, :].rearrange("p h t -> p (h t)"),
                                           kg[:, LIN_KEYS[n], :], start=True, stop=True)
                    mm.then_inc(lin_made[half], 1)
                pe.transpose(turn_bank[0][:, 0:P], kg[:, STATE_KEYS, :], ident).then_inc(k2_turned, 1)

                def make_state():
                    pe.wait_ge(k2_copied, u + 1)
                    pe.matmul(turn_bank[1][:, 0:D], k2[:, :], vu[:, 0, :], start=True, stop=True).then_inc(state_made, 1)

                pe.wait_ge(masked[0], u + 1)
                pe.wait_ge(masked[1], u + 1)
                if first:
                    make_state()
                else:
                    pb = (b - 1) % B
                    output(u - 1, pb, (g + 1) * GRP if pb == 0 else None, make_state)
                pe.wait_ge(state_copied, u + 1)
                for half in range(2):
                    pe.wait_ge(mixed[half], u + 1)
                    for r in range(4):
                        t = pe.transpose(turn_bank[half][:, r * P:(r + 1) * P], mix[:, 4 * half + r, :], ident)
                    t.then_inc(m_turned[half], 1)
                for n, half_cols in ((2, slice(0, 2 * P)), (3, slice(2 * P, 4 * P))):
                    pe.matmul(lin_bank[1][:, half_cols], state[:, n - 2, :],
                              qg[:, n, :, :], start=n == 2, stop=False, skip_group_check=True)
                pe.wait_ge(m_copied[0], u + 1)
                pe.matmul(lin_bank[0][:, :], vu[:, 0, :], mT[:, 0:4, :], start=True, stop=True).then_inc(pv_made[0], 1)
                pe.wait_ge(m_copied[1], u + 1)
                pe.wait_ge(v_mixed, u + 1)
                pe.matmul(lin_bank[1][:, 0:2 * P], vmix[:, :], mT[:, 4:6, :], start=False, stop=False, skip_group_check=True)
                pe.matmul(lin_bank[1][:, 2 * P:4 * P], vu[:, 1, :], mT[:, 6:8, :], start=False, stop=True,
                          skip_group_check=True).then_inc(pv_made[1], 1)

            over_units(pe, step)
            for tile in range(TT):
                pe.wait_ge(m_copied[tile], UNITS)
                turn_norm(2, tile)
            for tile in range(TT):
                pe.wait_ge(out_added[tile], UNITS - 1)
            output(UNITS - 1, B - 1, None)
            for tile in range(TT):
                pe.wait_ge(out_added[tile], UNITS)
            for i in range(TOK):
                if i + TT < TOK:
                    turn_norm(2, i + TT)
                ffn(TOK + i)

        @block.scalar
        def _(act):
            def root(r, i, n=1):
                act.wait_ge(eps_added[r], i + n)
                act.activation(dev[:, i:i + n], meanvar[:, i:i + n, 1], ACT.Sqrt).then_inc(dev_made[r], n)

            def copy_norm(r, i):
                act.wait_ge(xn_turned[r], i + 1)
                if r == 1:
                    act.wait_ge(ffn_made, i + 1)
                act.activation(xt_hi[:, :, i * P:(i + 1) * P],
                               norm_bank[r][i % 2][:, :].rearrange("p (k t) -> p k t", k=KT),
                               ACT.Copy).then_inc(xt_hi_made[r], 1)

            def split_chunk(g, k, par):
                act.wait_ge(w_in[k % 2], (g * 2 + (k // 2 + 1)) * 48)
                act.activation(w_hi[par][:, k, :], w_raw[k % 2][:, :], ACT.Copy).then_inc(w_hi_ready, 1)

            act.wait_ge(lb_turned, 1)
            act.activation(lbT, bank[0][0:R, :], ACT.Copy).then_inc(lb_copied, 1)
            for c in range(KT):
                act.wait_ge(eff_made, c + 1)
                if c >= 2:
                    act.wait_ge(squared, c - 1)
                act.activation(squares[c % 2], eff[:, c, :], ACT.Square, accum_out=norm2[:, c:c + 1]).then_inc(squared, 1)
            act.wait_ge(squared, KT)
            act.activation(colscale[:, :], norm2[:, :], ACT.Sqrt).then_inc(rooted, 1)
            for i in range(0, TOK, TOK // 2):
                root(0, i, TOK // 2)
            for k in range(KT):
                if k < 2:
                    split_chunk(0, k, 0)
            act.wait_ge(fwt_turned, KT)
            for k in range(KT):
                act.activation(ff_hi[0][:, k, :], bank[k][:, :], ACT.Copy).then_inc(fw_hi_ready, 1)
            for i in range(TOK + 2):
                if i < TOK:
                    copy_norm(0, i)
                if i == 1:
                    for k in range(KT):
                        act.wait_ge(fw_lo_ready, k + 1)
                        act.activation(fwt[:, k, :], bank[k][:, :], ACT.Copy).then_inc(fwt_copied, 1)
                if 0 <= i - 2 < TOK:
                    root(1, i - 2)
                if i in (1, 2):
                    split_chunk(0, i + 1, 0)
                if 0 <= i - 4 < TOK - TT:
                    copy_norm(1, i - 4)

            def split_wo(g, h):
                act.wait_ge(wo_in, (g + 1) * 16)
                if not (isinstance(g, int) and g == 0):
                    act.wait_ge(out_made[1], g * B)
                act.activation(wo_hi[:, h, :], wo_raw[:, h, :], ACT.Copy).then_inc(wo_hi_ready, 1)

            def copy_projected(u, upar, tile, first=False):
                act.wait_ge(q_made[tile], u + 1)
                if not first:
                    act.wait_ge(rotated[tile], u)
                    act.wait_ge(es_made[tile], u)
                act.activation(qk[tile][:, 0:GRP, :].rearrange("p h d -> p (h d)"), q_bank[:, :], ACT.Copy)\
                   .then_inc(q_copied[tile], 1)
                act.wait_ge(kv_made[tile], u + 1)
                if not first:
                    act.wait_ge(kraw_turned, u)
                act.activation(qk[tile][:, GRP, :], kv_bank[:, 0:D], ACT.Copy)
                if not (isinstance(u, int) and u < 2):
                    act.wait_ge(pv_made[1], u - 1)
                    act.wait_ge(v_mixed, u - 1)
                act.activation(v[upar][:, tile, :], kv_bank[:, D:2 * D], ACT.Copy).then_inc(kv_copied[tile], 1)

            def exp_projected(u, tile, first=False):
                act.wait_ge(max_made[tile], u + 1)
                act.wait_ge(q_copied[tile], u + 1)
                act.wait_ge(kv_copied[tile], u + 1)
                if not first:
                    act.wait_ge(es_turned[tile], u)
                    act.wait_ge(ks_turned, u)
                    act.wait_ge(es_recip[tile], u)
                for h in range(HEADS):
                    a = act.activation(es[tile][:, h, :], qk[tile][:, h, :], ACT.Exp, bias=nmax[tile][:, h:h + 1],
                                       accum_out=esum[tile][:, h:h + 1])
                a.then_inc(es_made[tile], 1)

            act.preload_act_table_set("natural_log_exp_and_others")
            for tile in range(TT):
                copy_projected(0, 0, tile, first=True)
                copy_norm(1, TOK - TT + tile)
            for tile in range(TT):
                exp_projected(0, tile, first=True)

            def step(g, b, first, last, odd=False, last_group=False):
                u = g * B + b
                par = int(odd)
                act.wait_ge(kraw_turned, u + 1)
                if not first:
                    act.wait_ge(logs_made, u)
                act.activation(krawT[:, :], q_bank[:, 0:N], ACT.Copy).then_inc(kraw_copied, 1)
                act.wait_ge(kr_turned, u + 1)
                if not first:
                    act.wait_ge(scored[1], u)
                act.activation(krT[:, :], kv_bank[:, 0:N], ACT.Copy).then_inc(kr_copied, 1)
                act.wait_ge(abs_made, u + 1)
                act.activation(lnk[:, :], lnk[:, :], ACT.Exp).then_inc(kexp_made, 1)
                for tile in range(TT):
                    act.wait_ge(qr_turned[tile], u + 1)
                    if not first:
                        act.wait_ge(scored[tile], u)
                    act.activation(qrT[:, 2 * tile:2 * tile + 2, :, :].rearrange("p n h t -> p h n t"),
                                   turn_bank[tile][:, :].rearrange("p (h n t) -> p h n t", h=GRP, n=2), ACT.Copy)\
                       .then_inc(qr_copied[tile], 1)
                    if tile == 0:
                        act.wait_ge(kexp_made, u + 1)
                        act.activation(lnk[:, :], lnk[:, :], ACT.Ln, bias=1.0).then_inc(kln_made, 1)
                if b == 1:
                    split_wo(g, 0)
                if not last:
                    copy_projected(u + 1, (b + 1) % 2, 0)
                act.wait_ge(dec_bounded, u + 1)
                act.activation(dec[:, :], dec[:, :], ACT.Exp, scale=1.0 / GATE_NORM).then_inc(gates_made, 1)
                if b == 1:
                    for h in range(1, GRP):
                        split_wo(g, h)
                act.wait_ge(ks_turned, u + 1)
                if not first:
                    act.wait_ge(kg_made, u)
                act.activation(ksT[:, :], kv_bank[:, 0:N], ACT.Copy).then_inc(ks_copied, 1)
                if not last:
                    exp_projected(u + 1, 0)
                for half in range(2):
                    act.wait_ge(masked[half], u + 1)
                    for r in range(4 * half, 4 * half + 4):
                        a = act.activation(sc[:, r, :], sc[:, r, :], ACT.Exp, scale=-1.0, bias=scmin[:, r:r + 1],
                                           accum_out=ssum[:, r:r + 1])
                    a.then_inc(e_made[half], 1)
                if not last:
                    copy_projected(u + 1, (b + 1) % 2, 1)
                act.wait_ge(k2_turned, u + 1)
                if not first:
                    act.wait_ge(state_made, u)
                act.activation(k2[:, :], turn_bank[0][:, 0:D], ACT.Copy).then_inc(k2_copied, 1)
                if not last_group:
                    for k in SPLIT_AT[b]:
                        split_chunk(g + 1, k, 1 - par)
                act.wait_ge(state_made, u + 1)
                act.wait_ge(gates_made, u + 1)
                if not first:
                    act.wait_ge(pv_made[1], u)
                act.activation(state[:, 0, :], turn_bank[1][:, 0:D], ACT.Copy)
                act.activation(state[:, 1, :], turn_bank[1][:, 0:D], ACT.Copy, scale=dec[:, DSTEP:DSTEP + 1])\
                   .then_inc(state_copied, 1)
                for half in range(2):
                    act.wait_ge(m_turned[half], u + 1)
                    if not first:
                        act.wait_ge(pv_made[half], u)
                    act.activation(mT[:, 4 * half:4 * half + 4, :].rearrange("p r q -> p (r q)"), turn_bank[half][:, :],
                                   ACT.Copy).then_inc(m_copied[half], 1)
                if not last:
                    exp_projected(u + 1, 1)
                if last_group:
                    act.activation(ff_hi[1][:, b, :], fwt[:, b, :], ACT.Copy).then_inc(fw_hi_ready, 1)
                for half in range(2):
                    act.wait_ge(pv_made[half], u + 1)
                    if not first:
                        act.wait_ge(o_ready[half], u)
                    act.activation(o_bf[:, half, :, :].rearrange("p h (n t) -> p h n t", n=2),
                                   lin_bank[half][:, :].rearrange("p (n h t) -> p h n t", n=2, h=GRP),
                                   ACT.Copy, scale=0.5).then_inc(o_copied[half], 1)

            over_units(act, step)
            root(2, 0, TOK - TT)
            for i in range(TOK):
                if i == TT:
                    for tile in range(TT):
                        root(2, TOK - TT + tile)
                copy_norm(2, i)

        @block.vector
        def _(dve):
            def statistics(r, i):
                if r == 0:
                    dve.wait_ge(x_in[i], 16)
                elif r == 1:
                    dve.wait_ge(ffn_added, i + 1)
                elif i >= TOK - TT:
                    dve.wait_ge(out_added[i % TT], UNITS)
                dve.bn_stats(stat[:, i, :], x[:, i, :]).then_inc(stats_made[r], 1)
                dve.wait_ge(stats_made[r], i + 1)
                if r >= 1:
                    dve.wait_ge(xn_made[r - 1], i + 1)
                dve.bn_aggr(meanvar[:, i, :], stat[:, i, :]).then_inc(aggregated[r], 1)
                dve.wait_ge(aggregated[r], i + 1)
                dve.tensor_scalar(meanvar[:, i, 1:2], meanvar[:, i, 1:2], EPS, None, ALU.add).then_inc(eps_added[r], 1)

            def invert_dev(r, i, n=1):
                dve.wait_ge(dev_made[r], i + n)
                dve.reciprocal(rstd[:, i:i + n], dev[:, i:i + n]).then_inc(rstd_made[r], n)

            def normalise(r, i):
                dve.wait_ge(rstd_made[r], i + 1)
                if i >= 2:
                    dve.wait_ge(xn_turned[r], i - 1)
                dve.tensor_scalar(xn[r % 2][i % 2], x[:, i, :], meanvar[:, i, 0:1], rstd[:, i:i + 1],
                                  ALU.subtract, ALU.mult).then_inc(xn_made[r], 1)

            def rest_norm(r, i):
                cols = slice(i * P, (i + 1) * P)
                dve.wait_ge(xt_hi_made[r], i + 1)
                dve.tensor_tensor(xt_lo[:, :, cols], norm_bank[r][i % 2][:, :].rearrange("p (k t) -> p k t", k=KT),
                                  xt_hi[:, :, cols].bitcast(F32), ALU.subtract).then_inc(xt_lo_made[r], 1)

            def add_ffn(f):
                dve.wait_ge(ffn_made, f + 1)
                dve.tensor_tensor(x[:, f % TOK, :], score_bank[f % 2][:, :], x[:, f % TOK, :], ALU.add)\
                   .then_inc(ffn_added, 1)

            for i in range(TOK // 2):
                statistics(0, i)
            dve.wait_ge(fw_in, 32)
            for c in range(KT):
                dve.wait_ge(ba_made, c + 1)
                dve.tensor_tensor(eff[:, c, :], bank[4 + c][:, :], fwt[:, c, :], ALU.add).then_inc(eff_made, 1)
            for i in range(TOK // 2, TOK - 1):
                statistics(0, i)
            dve.wait_ge(rooted, 1)
            dve.reciprocal(norm2[:, :], colscale[:, :]).then_inc(scaled_c, 1)
            dve.wait_ge(scaled_c, 1)
            dve.scalar_tensor_tensor(out=colscale[:, :], in0=norm2[:, :], scalar=0.5, in1=magc[:, :],
                                     op0=ALU.mult, op1=ALU.mult).then_inc(scaled_c, 1)
            dve.wait_ge(scaled_c, 2)
            for c in range(KT):
                dve.tensor_scalar(eff[:, c, :], eff[:, c, :], colscale[:, c:c + 1], None, ALU.mult).then_inc(eff_scaled, 1)
            invert_dev(0, 0, TOK // 2)
            normalise(0, 0)
            normalise(0, 1)
            statistics(0, TOK - 1)
            for k in range(KT):
                dve.wait_ge(fw_hi_ready, k + 1)
                dve.tensor_tensor(ff_lo[0][:, k, :], bank[k][:, :], ff_hi[0][:, k, :].bitcast(F32), ALU.subtract)\
                   .then_inc(fw_lo_ready, 1)
            for i in range(TOK + 2):
                if i < TOK:
                    rest_norm(0, i)
                if i == 1:
                    invert_dev(0, TOK // 2, TOK // 2)
                if 0 <= i - 2 < TOK:
                    add_ffn(i - 2)
                    statistics(1, i - 2)
                    invert_dev(1, i - 2)
                    normalise(1, i - 2)
                if 0 <= i - 4 < TOK - TT:
                    rest_norm(1, i - 4)

            def prepare(u, tile, first=False):
                dve.wait_ge(q_copied[tile], u + 1)
                dve.wait_ge(kv_copied[tile], u + 1)
                if not first:
                    dve.wait_ge(es_made[tile], u)
                dve.tensor_reduce(nmax[tile][:, :], qk[tile][:, :, :], AX_X, ALU.max, negate=True)\
                   .then_inc(max_made[tile], 1)
                if not first:
                    dve.wait_ge(roped[tile], u)
                    dve.wait_ge(kr_turned, u)
                    dve.wait_ge(qr_turned[tile], u)
                dve.tensor_tensor(rc[tile][:, :, :], qk[tile][:, :, :],
                                  cos[:, tile, :].unsqueeze(1).to_broadcast([P, HEADS, D]), ALU.mult)
                for a, b in ((0, D // 2), (D // 2, 0)):
                    r = dve.tensor_tensor(rs[tile][:, :, a:a + D // 2], qk[tile][:, :, b:b + D // 2],
                                          sin[:, tile, a:a + D // 2].unsqueeze(1).to_broadcast([P, HEADS, D // 2]),
                                          ALU.mult)
                r.then_inc(rotated[tile], 1)

            def invert(u, tile, first=False):
                dve.wait_ge(es_made[tile], u + 1)
                if not first:
                    dve.wait_ge(es_scaled[tile], u)
                dve.reciprocal(erec[tile][:, :], esum[tile][:, :]).then_inc(es_recip[tile], 1)

            def add_output(u, b):
                for tile in range(TT):
                    i = b * TT + tile
                    dve.wait_ge(out_made[tile], u + 1)
                    dve.tensor_tensor(x[:, i, :], score_bank[tile][:, :], x[:, i, :], ALU.add).then_inc(out_added[tile], 1)

            for tile in range(TT):
                prepare(0, tile, first=True)
                rest_norm(1, TOK - TT + tile)
            for tile in range(TT):
                invert(0, tile, first=True)

            def step(g, b, first, last, odd=False, last_group=False):
                u = g * B + b
                dve.wait_ge(kraw_copied, u + 1)
                dve.scalar_tensor_tensor(out=lnk[:, :], in0=krawT[:, :], scalar=-1.0, in1=krawT[:, :],
                                         op0=ALU.mult, op1=ALU.min).then_inc(abs_made, 1)
                dve.wait_ge(kv_copied[0], u + 1)
                dve.wait_ge(kv_copied[1], u + 1)
                if not first:
                    dve.wait_ge(pv_made[1], u)
                dve.tensor_copy(vmix[0:W, :], v[b % 2][0:W, 1, :])
                dve.tensor_copy(vmix[W:P, :], v[b % 2][W:P, 0, :]).then_inc(v_mixed, 1)
                dve.wait_ge(kln_made, u + 1)
                dve.scalar_tensor_tensor(out=logs[:, :], in0=krawT[:, :], scalar=0.0, in1=lnk[:, :],
                                         op0=ALU.min, op1=ALU.subtract).then_inc(logs_made, 1)
                dve.wait_ge(logs_made, u + 1)
                dve.tensor_tensor_scan(G[:, :], ones, logs[:, :], 0.0, ALU.mult, ALU.add).then_inc(summed, 1)
                dve.wait_ge(summed, u + 1)
                if not first:
                    dve.wait_ge(state_copied, u)
                mid = G[:, W // 2 - 1::W]
                dve.tensor_tensor(dec[:, 0:3 * P].rearrange("p (n s) -> p n s", n=3),
                                  mid[:, 0:3].unsqueeze(2).to_broadcast([P, 3, P]),
                                  G[:, 0:P].unsqueeze(1).to_broadcast([P, 3, P]), ALU.subtract)
                dve.tensor_tensor(dec[:, 3 * P:5 * P].rearrange("p (n s) -> p n s", n=2),
                                  mid[:, 2:4].unsqueeze(2).to_broadcast([P, 2, P]),
                                  G[:, P:2 * P].unsqueeze(1).to_broadcast([P, 2, P]), ALU.subtract)
                dve.tensor_tensor(dec[:, DQ:DSTEP].rearrange("p (n s) -> p n s", n=NB),
                                  G[:, :].rearrange("p (n s) -> p n s", n=NB),
                                  mid.unsqueeze(2).to_broadcast([P, NB, W]), ALU.subtract)
                dve.tensor_tensor(dec[:, DSTEP:DSTEP + 1], mid[:, 3:4], mid[:, 2:3], ALU.subtract).then_inc(dec_made, 1)
                dve.wait_ge(dec_made, u + 1)
                dve.tensor_scalar(dec[:, :], dec[:, :], MOST, None, ALU.min).then_inc(dec_bounded, 1)
                if not last:
                    prepare(u + 1, 0)
                for half in range(2):
                    dve.wait_ge(scored[half], u + 1)
                    dve.nop(nofuse=True)
                    for r in range(4 * half, 4 * half + 4):
                        m = dve.tensor_tensor_reduce(sc[:, r, :], score_bank[half][:, (r % 4) * P:(r % 4 + 1) * P],
                                                     win[:, WIN_OF_BLOCK[r // 2], :], -float(D) ** -0.5, BIG,
                                                     ALU.add, ALU.min, scmin[:, r:r + 1])
                    m.then_inc(masked[half], 1)
                dve.wait_ge(gates_made, u + 1)
                for tile in range(TT):
                    dve.wait_ge(es_turned[tile], u + 1)
                    if not first:
                        dve.wait_ge(lin_made[tile], u)
                        dve.wait_ge(pv_made[1], u)
                    dve.tensor_tensor(qg[:, 2 * tile:2 * tile + 2, :, :].rearrange("p n h t -> p h n t"),
                                      turn_bank[tile][:, :].rearrange("p (h n t) -> p h n t", h=GRP, n=2),
                                      dec[:, DQ + tile * P:DQ + (tile + 1) * P].rearrange("p (n t) -> p n t", n=2)
                                      .unsqueeze(1).to_broadcast([P, GRP, 2, W]),
                                      ALU.mult).then_inc(qg_made[tile], 1)
                dve.wait_ge(ks_copied, u + 1)
                if not first:
                    dve.wait_ge(lin_made[1], u)
                    dve.wait_ge(k2_turned, u)
                dve.tensor_tensor(kg[:, 0:3, :], ksT[:, 0:P].unsqueeze(1).to_broadcast([P, 3, P]),
                                  dec[:, 0:3 * P].rearrange("p (n s) -> p n s", n=3), ALU.mult)
                dve.tensor_tensor(kg[:, 3:5, :], ksT[:, P:2 * P].unsqueeze(1).to_broadcast([P, 2, P]),
                                  dec[:, 3 * P:5 * P].rearrange("p (n s) -> p n s", n=2), ALU.mult).then_inc(kg_made, 1)
                if not last:
                    invert(u + 1, 0)
                for half in range(2):
                    rows = slice(4 * half, 4 * half + 4)
                    dve.wait_ge(e_made[half], u + 1)
                    dve.reciprocal(srec[:, rows], ssum[:, rows]).then_inc(e_recip[half], 1)
                    dve.wait_ge(lin_made[half], u + 1)
                    if not first:
                        dve.wait_ge(m_turned[half], u)
                    dve.tensor_tensor(mix[:, rows, :].rearrange("p (n h) k -> p n h k", n=2),
                                      lin_bank[half][:, :].rearrange("p (n h k) -> p n h k", n=2, h=2),
                                      lin.unsqueeze(2).to_broadcast([P, 2, 2, P]), ALU.min).then_inc(lin_masked[half], 1)
                    dve.wait_ge(e_recip[half], u + 1)
                    dve.wait_ge(lin_masked[half], u + 1)
                    for r in range(4 * half, 4 * half + 4):
                        m = dve.scalar_tensor_tensor(out=mix[:, r, :], in0=sc[:, r, :], scalar=srec[:, r:r + 1],
                                                     in1=mix[:, r, :], op0=ALU.mult, op1=ALU.add)
                    m.then_inc(mixed[half], 1)
                if not last:
                    prepare(u + 1, 1)
                if not first:
                    add_output(u - 1, (b - 1) % B)
                if not last:
                    invert(u + 1, 1)

            over_units(dve, step)
            for i in range(TOK - TT):
                statistics(2, i)
            invert_dev(2, 0, TOK - TT)
            for tile in range(TT):
                normalise(2, tile)
            for tile in range(TT):
                rest_norm(2, tile)
            add_output(UNITS - 1, B - 1)
            for tile in range(TT):
                normalise(2, TT + tile)
            for tile in range(TT):
                statistics(2, TOK - TT + tile)
            for i in range(TT, TOK + 1):
                if i < TOK:
                    rest_norm(2, i)
                if i == TT:
                    for tile in range(TT):
                        invert_dev(2, TOK - TT + tile)
                if i + TT < TOK:
                    normalise(2, i + TT)
                add_ffn(TOK + i - TT)
            add_ffn(2 * TOK - 1)

        @block.gpsimd
        def _(pool):
            def split_chunk(g, k, par):
                pool.wait_ge(w_hi_ready, g * KT + (k + 1))
                pool.tensor_tensor(w_lo[par][:, k, :], w_raw[k % 2][:, :], w_hi[par][:, k, :].bitcast(F32), ALU.subtract)\
                    .then_inc(w_lo_ready, 1)

            def split_wo(g, h):
                pool.wait_ge(wo_hi_ready, g * GRP + (h + 1))
                pool.tensor_tensor(wo_lo[:, h, :], wo_raw[:, h, :], wo_hi[:, h, :].bitcast(F32), ALU.subtract)\
                    .then_inc(wo_lo_ready, 1)

            def rope(u, tile):
                pool.wait_ge(rotated[tile], u + 1)
                pool.tensor_tensor(rc[tile][:, :, :], rc[tile][:, :, :], rs[tile][:, :, :], ALU.add)\
                    .then_inc(roped[tile], 1)

            def scale(u, tile):
                pool.wait_ge(es_recip[tile], u + 1)
                pool.tensor_tensor(es[tile][:, :, :], es[tile][:, :, :],
                                   erec[tile][:, :].unsqueeze(2).to_broadcast([P, HEADS, D]), ALU.mult)\
                    .then_inc(es_scaled[tile], 1)

            split_chunk(0, 0, 0)
            split_chunk(0, 1, 0)
            for i in range(2, TOK):
                pool.wait_ge(rstd_made[0], TOK // 2 if i < TOK // 2 else TOK)
                pool.wait_ge(xn_made[0], i)
                pool.wait_ge(xn_turned[0], i - 1)
                pool.tensor_scalar(xn[0][i % 2], x[:, i, :], meanvar[:, i, 0:1], rstd[:, i:i + 1],
                                   ALU.subtract, ALU.mult).then_inc(xn_made[0], 1)
                if i in (4, 5):
                    split_chunk(0, i - 2, 0)
            for tile in range(TT):
                rope(0, tile)
                scale(0, tile)

            def step(g, b, first, last, odd=False, last_group=False):
                u = g * B + b
                par = int(odd)
                if b == 1:
                    split_wo(g, 0)
                if not last:
                    rope(u + 1, 0)
                if b == 1:
                    split_wo(g, 1)
                    split_wo(g, 2)
                if not last:
                    scale(u + 1, 0)
                if b == 1:
                    split_wo(g, 3)
                if not last_group:
                    for k in SPLIT_AT[b]:
                        split_chunk(g + 1, k, 1 - par)
                if not last:
                    rope(u + 1, 1)
                    scale(u + 1, 1)
                for half in range(2):
                    pool.wait_ge(o_copied[half], u + 1)
                    if not first:
                        pool.wait_ge(out_made[half], u)
                    pool.nop(nofuse=True)
                    pool.tensor_copy(o_r[:, half, :, :], o_bf[:, half, :, :]).then_inc(o_ready[half], 1)
                if last_group:
                    pool.wait_ge(fw_hi_ready, KT + b + 1)
                    pool.tensor_tensor(ff_lo[1][:, b, :], fwt[:, b, :], ff_hi[1][:, b, :].bitcast(F32), ALU.subtract)\
                        .then_inc(fw_lo_ready, 1)

            over_units(pool, step)


def shape_constants():
    import numpy as np
    c = np.zeros((P, C_ALL), np.float32)
    half = np.arange(D // 2, dtype=np.float32)
    inv = np.float32(1.0) / np.power(np.float32(10000.0), np.float32(2.0) * half / np.float32(D))
    fr = np.arange(N, dtype=np.float32)[:, None] * inv[None, :].astype(np.float32)
    cos, sin = np.cos(fr), np.sin(fr)
    for t in range(TT):
        rows = slice(t * P, (t + 1) * P)
        c[:, C_COS + t * D:C_COS + (t + 1) * D] = np.concatenate([cos[rows], cos[rows]], 1)
        c[:, C_SIN + t * D:C_SIN + (t + 1) * D] = np.concatenate([-sin[rows], sin[rows]], 1)
    t = np.arange(P)[:, None] % W
    k = np.arange(P)[None, :]
    own, back = k % W <= t, k % W >= t
    early = k < W
    windows = (early & own, (early & back) | (~early & own), (early & own) | (~early & back))
    for i, seen in enumerate(windows):
        c[:, C_WIN + i * P:C_WIN + (i + 1) * P] = np.where(seen, 0.0, FAR)
    for i, seen in enumerate((early & own, early | own)):
        c[:, C_LIN + i * P:C_LIN + (i + 1) * P] = np.where(seen, BIG, 0.0)
    c[:, C_ID:C_ONE] = np.eye(P)
    c[:, C_ONE:] = 1.0
    return c


def kernel(L0_attn_hidden_states, L0_attn_Wq, L0_attn_Wk, L0_attn_Wv, L0_attn_Wo, L0_ffn_W, L0_ffn_lora_A,
           L0_ffn_lora_B, L0_ffn_magnitude):
    import numpy as np
    import concourse.bacc as bacc
    from concourse.bass_utils import run_bass_kernel_spmd

    nc = bacc.Bacc("TRN2", target_bir_lowering=False, num_devices=1)
    arrays = {
        "hs": np.ascontiguousarray(L0_attn_hidden_states).reshape(B * N, HID),
        "wq": L0_attn_Wq, "wk": L0_attn_Wk, "wv": L0_attn_Wv, "wo": L0_attn_Wo,
        "fw": L0_ffn_W, "la": L0_ffn_lora_A, "lb": L0_ffn_lora_B,
        "mag": np.asarray(L0_ffn_magnitude).reshape(KT, P).T,
        "consts": shape_constants(),
    }
    arrays = {f"{name}_dram": np.ascontiguousarray(a) for name, a in arrays.items()}
    args = [nc.dram_tensor(name, a.shape, mybir.dt.from_np(a.dtype), kind="ExternalInput").ap()
            for name, a in arrays.items()]
    args.append(nc.dram_tensor("out_dram", (B * N, HID), F32, kind="ExternalOutput").ap())
    layer_program(nc, *args)
    r = run_bass_kernel_spmd(nc, [arrays], core_ids=[0])
    return r.results[0]["out_dram"].reshape(B, N, HID)
```

```python
from contextlib import ExitStack

import concourse.bass as bass
from concourse import mybir

P = 128
B, N, HID = 4, 256, 512
H, KVH, D, W = 32, 8, 128, 64
R = 32
GRP = H // KVH
HEADS = GRP + 1
KT = HID // P
TOK = B * N // P
TT = N // P
NB = N // W
QW = GRP * D
UNITS = KVH * B
EPS = 1e-5
GATE_NORM = 16.0
MOST = 85.0 * GATE_NORM
FAR = -1.0e30
BIG = 3.0e38

F32 = mybir.dt.float32
F32R = mybir.dt.float32r
BF16 = mybir.dt.bfloat16
ALU = mybir.AluOpType
ACT = mybir.ActivationFunctionType
AX_X = mybir.AxisListType.X

KEYS = 5
DQ = KEYS * P
DSTEP = DQ + N
LIN_KEYS = (0, 1, 3, 4)
STATE_KEYS = 2

C_COS, C_SIN, C_WIN, C_LIN, C_ID, C_ONE = 0, TT * D, 2 * TT * D, 2 * TT * D + 3 * P, 2 * TT * D + 5 * P, 2 * TT * D + 6 * P
C_ALL = C_ONE + 1
SPLIT_AT = ((0,), (1,), (2, 3), ())
WIN_OF_BLOCK = (0, 1, 2, 1)
WIN_COLS = (W, P, P, P)
LIN_COLS = (W, P, W, P)
WIN_KEYS = (slice(0, 1), slice(0, 3, 2), slice(1, 3), slice(1, 4, 2))


def layer_program(nc, hs, wq, wk, wv, wo, fw, la, lb, mag, consts, out):
    ctx = ExitStack()
    with ctx:
        def sb(name, shape, dt=F32):
            return ctx.enter_context(nc.sbuf_tensor(name, shape, dt))

        def sem(name):
            return ctx.enter_context(nc.semaphore(name))

        def sems(name, n=2):
            return [sem(f"{name}{i}") for i in range(n)]

        x = sb("x", [P, TOK, HID])
        xt_hi = sb("xt_hi", [P, KT, TOK * P], F32R)
        xt_lo = sb("xt_lo", [P, KT, TOK * P], F32R)
        w_hi = [sb(f"w_hi{i}", [P, KT, QW + 2 * D], F32R) for i in range(2)]
        w_lo = [sb(f"w_lo{i}", [P, KT, QW + 2 * D], F32R) for i in range(2)]
        w_raw = [sb(f"w_raw{i}", [P, QW + 2 * D]) for i in range(2)]
        wo_hi = sb("wo_hi", [P, GRP, HID], F32R)
        wo_lo = sb("wo_lo", [P, GRP, HID], F32R)
        wo_raw = sb("wo_raw", [P, 2, HID])
        fwt = sb("fwt", [P, KT, HID])
        cst = sb("cst", [P, C_ALL])
        qk = [sb(f"qk{i}", [P, HEADS, D]) for i in range(TT)]
        rc = [sb(f"rc{i}", [P, HEADS, D]) for i in range(TT)]
        rs = [sb(f"rs{i}", [P, HEADS, D]) for i in range(TT)]
        es = [sb(f"es{i}", [P, HEADS, D]) for i in range(TT)]
        v = [sb(f"v{i}", [P, TT, D]) for i in range(2)]
        v_hi = sb("v_hi", [P, TT, D], F32R)
        v_lo = sb("v_lo", [P, TT, D], F32R)
        vmix_hi = sb("vmix_hi", [P, D], F32R)
        vmix_lo = sb("vmix_lo", [P, D], F32R)
        krawT = sb("krawT", [P, N])
        krT = sb("krT", [P, NB, W])
        ksT = sb("ksT", [P, N])
        lnk = sb("lnk", [P, N])
        G = krawT
        dec = sb("dec", [P, DSTEP + 1])
        kg = sb("kg", [P, KEYS, P])
        qrT = sb("qrT", [P, NB, GRP, W])
        qg = sb("qg", [P, NB, GRP, W])
        k2 = sb("k2", [P, D])
        state = sb("state", [P, 2, D])
        sc = sb("sc", [P, 8, P])
        mix = sb("mix", [P, 8, P])
        mT_hi = sb("mT_hi", [P, 8, P], F32R)
        mT_lo = sb("mT_lo", [P, 8, P], F32R)
        o_bf = sb("o_bf", [P, TT, GRP, P], BF16)
        o_r = sb("o_r", [P, TT, GRP, P], F32R)
        nmax = [sb(f"nmax{i}", [P, HEADS]) for i in range(TT)]
        esum = [sb(f"esum{i}", [P, HEADS]) for i in range(TT)]
        erec = [sb(f"erec{i}", [P, HEADS]) for i in range(TT)]
        scmin = sb("scmin", [P, 8])
        ssum = sb("ssum", [P, 8])
        srec = sb("srec", [P, 8])
        stat = sb("stat", [P, TOK, 6])
        meanvar = sb("meanvar", [P, TOK, 2])
        dev = sb("dev", [P, TOK])
        rstd = sb("rstd", [P, TOK])
        magc = sb("magc", [P, KT])
        norm2 = sb("norm2", [P, KT])
        colscale = sb("colscale", [P, KT])
        first_half, second_half = slice(0, 4), slice(4, 8)
        xn = [[t[:, hf, :].rearrange("p a b -> p (a b)") for hf in (first_half, second_half)] for t in (sc, mix)]
        squares = [qk[i][:, 0:GRP, :].rearrange("p a b -> p (a b)") for i in range(TT)]
        eff = [t[:, 0:GRP, :].rearrange("p a b -> p (a b)") for t in rc + rs]
        ff_hi = [w_hi[i][:, :, 0:HID] for i in (1, 0)]
        ff_lo = [w_lo[i][:, :, 0:HID] for i in (1, 0)]
        lbT = qrT[0:R, 0:2, :, :].rearrange("p a b c -> p (a b c)")
        la_sb = qrT[0:R, 2:4, :, :].rearrange("p a b c -> p (a b c)")
        lb_sb = k2[:, :].rearrange("p (c r) -> p c r", r=R)

        cos = cst[:, C_COS:C_SIN].rearrange("p (t d) -> p t d", d=D)
        sin = cst[:, C_SIN:C_WIN].rearrange("p (t d) -> p t d", d=D)
        win = cst[:, C_WIN:C_LIN].rearrange("p (n k) -> p n k", k=P)
        lin = cst[:, C_LIN:C_ID].rearrange("p (n k) -> p n k", k=P)
        ident = cst[:, C_ID:C_ONE]
        ones = cst[:, C_ONE:C_ALL].to_broadcast([P, N])

        bank = [ctx.enter_context(nc.psum_tensor(f"bank{i}", [P, 512], F32)) for i in range(8)]
        q_bank, kv_bank = bank[0], bank[1]
        norm_bank = (bank[6:8], bank[2:4], bank[2:4])
        turn_bank = bank[2:4]
        score_bank = bank[4:6]
        lin_bank = bank[6:8]

        x_in = sems("x_in", TOK)
        ident_in, tables_in, fw_in, lora_in = sem("ident_in"), sem("tables_in"), sem("fw_in"), sem("lora_in")
        lb_turned, lb_copied, ba_made, eff_made = sem("lb_turned"), sem("lb_copied"), sem("ba_made"), sem("eff_made")
        squared, rooted, scaled_c, eff_scaled = sem("squared"), sem("rooted"), sem("scaled_c"), sem("eff_scaled")
        fwt_turned, fwt_copied = sem("fwt_turned"), sem("fwt_copied")
        fw_hi_ready, fw_lo_ready = sem("fw_hi_ready"), sem("fw_lo_ready")
        stats_made, aggregated, eps_added = sems("stats_made", 3), sems("aggregated", 3), sems("eps_added", 3)
        dev_made, rstd_made, xn_made = sems("dev_made", 3), sems("rstd_made", 3), sems("xn_made", 3)
        xn_turned, xt_hi_made, xt_lo_made = sems("xn_turned", 3), sems("xt_hi_made", 3), sems("xt_lo_made", 3)
        ffn_made, ffn_added, stored = sem("ffn_made"), sem("ffn_added"), sem("stored")

        w_in = sems("w_in")
        wo_in = sems("wo_in")
        w_hi_ready, w_lo_ready = sem("w_hi_ready"), sem("w_lo_ready")
        wo_hi_ready, wo_lo_ready = sem("wo_hi_ready"), sem("wo_lo_ready")

        q_made, kv_made = sems("q_made"), sems("kv_made")
        q_copied, kv_copied = sems("q_copied"), sems("kv_copied")
        max_made, rotated, roped = sems("max_made"), sems("rotated"), sems("roped")
        es_made, es_recip, es_scaled = sems("es_made"), sems("es_recip"), sems("es_scaled")
        v_hi_made, v_lo_made, v_mixed = sem("v_hi_made"), sem("v_lo_made"), sem("v_mixed")
        kraw_turned, kr_turned, ks_turned = sem("kraw_turned"), sem("kr_turned"), sem("ks_turned")
        kraw_copied, kr_copied, ks_copied = sem("kraw_copied"), sem("kr_copied"), sem("ks_copied")
        qr_turned, qr_copied, es_turned = sems("qr_turned"), sems("qr_copied"), sems("es_turned")
        abs_made, kexp_made, kln_made = sem("abs_made"), sem("kexp_made"), sem("kln_made")
        logs_made, summed, dec_made, dec_bounded, gates_made = (
            sem("logs_made"), sem("summed"), sem("dec_made"), sem("dec_bounded"), sem("gates_made"))
        kg_made, qg_made = sem("kg_made"), sems("qg_made")
        k2_turned, k2_copied, state_made, state_copied = (
            sem("k2_turned"), sem("k2_copied"), sem("state_made"), sem("state_copied"))
        scored, masked, e_made, e_recip = sems("scored"), sems("masked"), sems("e_made"), sems("e_recip")
        lin_made, lin_masked, mixed = sems("lin_made"), sems("lin_masked"), sems("mixed")
        m_turned, m_copied, m_lo_made, pv_made, o_copied, o_ready = (
            sems("m_turned"), sems("m_copied"), sems("m_lo_made"), sems("pv_made"), sems("o_copied"), sems("o_ready"))
        out_made, out_added = sems("out_made"), sems("out_added")

        def over_units(eng, step):
            for b in range(B):
                step(0, b, first=b == 0, last=False)
            with eng.Fori(1, KVH - 1, 2) as g:
                for b in range(B):
                    step(g, b, first=False, last=False, odd=True)
                for b in range(B):
                    step(g + 1, b, first=False, last=False)
            for b in range(B):
                step(KVH - 1, b, first=False, last=b == B - 1, odd=True, last_group=True)

        block = ctx.enter_context(nc.Block())

        @block.sync
        def _(sp):
            sp.dma_start(cst[:, C_ID:], consts[:, C_ID:]).then_inc(ident_in, 16)
            sp.dma_start(lb_sb, lb.rearrange("(c p) r -> p c r", p=P)).then_inc(lora_in, 16)
            sp.dma_start(la_sb, la).then_inc(lora_in, 16)
            sp.dma_start(fwt[:, :, :], fw.rearrange("(c p) i -> p c i", p=P)).then_inc(fw_in, 16)
            sp.dma_start(magc[:, :], mag).then_inc(fw_in, 16)
            for i in range(TOK):
                sp.dma_start(x[:, i, :], hs[i * P:(i + 1) * P, :]).then_inc(x_in[i], 16)
                if i == TOK // 2 - 1:
                    sp.dma_start(cst[:, 0:C_ID], consts[:, 0:C_ID]).then_inc(tables_in, 16)

            def load_chunk(g, k):
                s = k % 2
                rows = slice(k * P, (k + 1) * P)
                sp.dma_start(w_raw[s][:, 0:QW], wq[rows, bass.ds(g * QW, QW)]).then_inc(w_in[s], 16)
                sp.dma_start(w_raw[s][:, QW:QW + D], wk[rows, bass.ds(g * D, D)]).then_inc(w_in[s], 16)
                sp.dma_start(w_raw[s][:, QW + D:], wv[rows, bass.ds(g * D, D)]).then_inc(w_in[s], 16)

            def load_wo(g, h):
                sp.dma_start(wo_raw[:, h % 2, :], wo[bass.ds((g * GRP + h) * D, D), :]).then_inc(wo_in[h % 2], 16)

            for k in range(KT):
                if k >= 2:
                    sp.wait_ge(w_hi_ready, k - 1)
                    sp.wait_ge(w_lo_ready, k - 1)
                load_chunk(0, k)
            load_wo(0, 0)
            load_wo(0, 1)
            with sp.Fori(1, KVH) as g:
                for k in range(KT):
                    if k == KT - 1:
                        for h in (2, 3):
                            sp.wait_ge(wo_hi_ready, g * GRP + (h - 1 - GRP))
                            sp.wait_ge(wo_lo_ready, g * GRP + (h - 1 - GRP))
                            load_wo(g - 1, h)
                    sp.wait_ge(w_hi_ready, g * KT + (k - 1))
                    sp.wait_ge(w_lo_ready, g * KT + (k - 1))
                    load_chunk(g, k)
                for h in (0, 1):
                    sp.wait_ge(wo_hi_ready, g * GRP + (h - 1))
                    sp.wait_ge(wo_lo_ready, g * GRP + (h - 1))
                    load_wo(g, h)
            for h in (2, 3):
                sp.wait_ge(wo_hi_ready, (KVH - 1) * GRP + h - 1)
                sp.wait_ge(wo_lo_ready, (KVH - 1) * GRP + h - 1)
                load_wo(KVH - 1, h)
            for i in range(TOK):
                sp.wait_ge(ffn_added, TOK + i + 1)
                sp.dma_start(out[i * P:(i + 1) * P, :], x[:, i, :]).then_inc(stored, 16)
            sp.wait_ge(stored, 16 * TOK)

        @block.tensor
        def _(pe):
            def three(dst, a_hi, a_lo, b_hi, b_lo, start, stop):
                pe.matmul(dst, a_hi, b_hi, start=start, stop=False)
                pe.matmul(dst, a_hi, b_lo, start=False, stop=False)
                return pe.matmul(dst, a_lo, b_hi, start=False, stop=stop)

            def turn_norm(r, i):
                pe.wait_ge(xn_made[r], i + 1)
                if i >= 2:
                    pe.wait_ge(xt_lo_made[r], i - 1)
                for k in range(KT):
                    t = pe.transpose(norm_bank[r][i % 2][:, k * P:(k + 1) * P], xn[r % 2][i % 2][:, k * P:(k + 1) * P],
                                     ident)
                t.then_inc(xn_turned[r], 1)

            def ffn(f):
                i, second = f % TOK, f // TOK
                pe.wait_ge(xt_hi_made[2 * second], i + 1)
                pe.wait_ge(xt_lo_made[2 * second], i + 1)
                if i >= 2:
                    pe.wait_ge(ffn_added, f - 1)
                for k in range(KT):
                    if i == 0:
                        pe.wait_ge(fw_hi_ready, second * KT + k + 1)
                        pe.wait_ge(fw_lo_ready, second * KT + k + 1)
                    cols = slice(i * P, (i + 1) * P)
                    mm = three(score_bank[f % 2][:, :], xt_hi[:, k, cols], xt_lo[:, k, cols],
                               ff_hi[second][:, k, :], ff_lo[second][:, k, :], k == 0, k == KT - 1)
                mm.then_inc(ffn_made, 1)

            pe.wait_ge(ident_in, 16)
            pe.wait_ge(lora_in, 32)
            for c in range(KT):
                t = pe.transpose(bank[0][0:R, c * P:(c + 1) * P], lb_sb[:, c, :], ident)
            t.then_inc(lb_turned, 1)
            pe.wait_ge(lb_copied, 1)
            for c in range(KT):
                pe.matmul(bank[4 + c][:, :], lbT[:, c * P:(c + 1) * P], la_sb, start=True, stop=True).then_inc(ba_made, 1)
            for c in range(KT):
                pe.wait_ge(eff_scaled, c + 1)
                for k in range(KT):
                    t = pe.transpose(bank[k][:, c * P:(c + 1) * P], eff[c][:, k * P:(k + 1) * P], ident)
                t.then_inc(fwt_turned, 1)
            turn_norm(0, 0)
            turn_norm(0, 1)

            def project(u, b, tile, wpar, new_weights, first=False):
                if new_weights is not None:
                    pe.wait_ge(w_hi_ready, new_weights)
                    pe.wait_ge(w_lo_ready, new_weights)
                i = b * TT + tile
                cols = slice(i * P, (i + 1) * P)
                if first:
                    pe.wait_ge(xt_hi_made[1], tile + 1)
                    pe.wait_ge(xt_lo_made[1], tile + 1)
                if tile == 1:
                    pe.wait_ge(q_copied[0], u + 1)
                elif not first:
                    pe.wait_ge(kraw_copied, u)
                for k in range(KT):
                    mm = three(q_bank[:, :], xt_hi[:, k, cols], xt_lo[:, k, cols],
                               w_hi[wpar][:, k, 0:QW], w_lo[wpar][:, k, 0:QW], k == 0, k == KT - 1)
                mm.then_inc(q_made[tile], 1)
                if tile == 0 and not first:
                    pe.wait_ge(kr_copied, u)
                if tile == 1 and not first:
                    pe.wait_ge(ks_copied, u)
                if tile == 1 and first:
                    pe.wait_ge(kv_copied[0], u + 1)
                for k in range(KT):
                    mm = three(kv_bank[:, 0:2 * D], xt_hi[:, k, cols], xt_lo[:, k, cols],
                               w_hi[wpar][:, k, QW:], w_lo[wpar][:, k, QW:], k == 0, k == KT - 1)
                mm.then_inc(kv_made[tile], 1)

            def output(u, b, wo_count, between=None):
                if b == 0:
                    pe.wait_ge(wo_hi_ready, wo_count)
                    pe.wait_ge(wo_lo_ready, wo_count)
                for tile in range(TT):
                    pe.wait_ge(o_ready[tile], u + 1)
                    for h in range(GRP):
                        pe.matmul(score_bank[tile][:, :], o_r[:, tile, h, :], wo_hi[:, h, :], start=h == 0, stop=False)
                        mm = pe.matmul(score_bank[tile][:, :], o_r[:, tile, h, :], wo_lo[:, h, :], start=False,
                                       stop=h == GRP - 1)
                    mm.then_inc(out_made[tile], 1)
                    if tile == 0 and between:
                        between()

            for i in range(2, TOK):
                ffn(i - 2)
                turn_norm(0, i)
                if i == 3:
                    pe.wait_ge(fwt_copied, KT)
                if i >= 4:
                    turn_norm(1, i - 4)
            ffn(TOK - 2)
            turn_norm(1, TOK - 4)
            project(0, 0, 0, 0, KT, first=True)
            ffn(TOK - 1)
            turn_norm(1, TOK - 3)
            project(0, 0, 1, 0, None, first=True)
            for i in range(TOK - TT, TOK):
                turn_norm(1, i)

            def turn_kraw(u):
                pe.wait_ge(kv_copied[0], u + 1)
                pe.wait_ge(kv_copied[1], u + 1)
                for tile in range(TT):
                    t = pe.transpose(q_bank[:, tile * P:(tile + 1) * P], qk[tile][:, GRP, :], ident)
                t.then_inc(kraw_turned, 1)

            turn_kraw(0)

            def step(g, b, first, last, odd=False, last_group=False):
                u = g * B + b
                par = int(odd)
                nb, npar = (b + 1, par) if b + 1 < B else (0, 1 - par)
                vu = v[b % 2]
                pe.wait_ge(roped[0], u + 1)
                pe.wait_ge(roped[1], u + 1)
                for tile in range(TT):
                    t = pe.transpose(kv_bank[:, tile * P:(tile + 1) * P], rc[tile][:, GRP, :], ident)
                t.then_inc(kr_turned, 1)
                if first:
                    for r in range(TT, TOK):
                        pe.wait_ge(xt_hi_made[1], r + 1)
                        pe.wait_ge(xt_lo_made[1], r + 1)
                for tile in range(TT):
                    if not first:
                        pe.wait_ge(m_lo_made[tile], u)
                    for h in range(GRP):
                        t = pe.transpose(turn_bank[tile][:, h * P:(h + 1) * P], rc[tile][:, h, :], ident)
                    t.then_inc(qr_turned[tile], 1)
                if not last:
                    project(u + 1, nb, 0, npar, (g + 2) * KT if b == B - 1 else None)
                for half in range(2):
                    pe.wait_ge(qr_copied[half], u + 1)
                    if not (isinstance(u, int) and u < 2):
                        pe.wait_ge(out_added[half], u - 1)
                    for n in (2 * half, 2 * half + 1):
                        for hp in range(2):
                            r = (n * 2 + hp) % 4
                            q = qrT[:, n, 2 * hp:2 * hp + 2, :].rearrange("p h t -> p (h t)")
                            mm = pe.matmul(score_bank[half][:, r * P:r * P + WIN_COLS[n]], q, krT[:, WIN_KEYS[n], :],
                                           start=True, stop=True)
                    mm.then_inc(scored[half], 1)
                for tile in range(TT):
                    pe.wait_ge(es_scaled[tile], u + 1)
                    for h in range(GRP):
                        t = pe.transpose(turn_bank[tile][:, h * P:(h + 1) * P], es[tile][:, h, :], ident)
                    t.then_inc(es_turned[tile], 1)
                if last:
                    pe.wait_ge(kr_copied, u + 1)
                else:
                    pe.wait_ge(kv_copied[0], u + 2)
                for tile in range(TT):
                    t = pe.transpose(kv_bank[:, tile * P:(tile + 1) * P], es[tile][:, GRP, :], ident)
                t.then_inc(ks_turned, 1)
                if not last:
                    project(u + 1, nb, 1, npar, None)
                if last:
                    for tile in range(TT):
                        pe.wait_ge(masked[tile], u + 1)
                    output(u - 1, (b - 1) % B, None)
                pe.wait_ge(kg_made, u + 1)
                for half in range(2):
                    pe.wait_ge(qg_made[half], u + 1)
                    if not first:
                        pe.wait_ge(o_copied[half], u)
                    for n in (2 * half, 2 * half + 1):
                        for hp in range(2):
                            r = (n * 2 + hp) % 4
                            mm = pe.matmul(lin_bank[half][:, r * P:r * P + LIN_COLS[n]],
                                           qg[:, n, 2 * hp:2 * hp + 2, :].rearrange("p h t -> p (h t)"),
                                           kg[:, LIN_KEYS[n], 0:LIN_COLS[n]], start=True, stop=True)
                    mm.then_inc(lin_made[half], 1)
                pe.transpose(turn_bank[0][:, 0:P], kg[:, STATE_KEYS, :], ident).then_inc(k2_turned, 1)

                def make_state():
                    pe.wait_ge(k2_copied, u + 1)
                    pe.matmul(turn_bank[1][:, 0:D], k2[:, :], vu[:, 0, :], start=True, stop=True).then_inc(state_made, 1)

                pe.wait_ge(masked[0], u + 1)
                pe.wait_ge(masked[1], u + 1)
                if first or last:
                    make_state()
                else:
                    pb = (b - 1) % B
                    output(u - 1, pb, (g + 1) * GRP if pb == 0 else None, make_state)
                pe.wait_ge(state_copied, u + 1)
                for half in range(2):
                    pe.wait_ge(mixed[half], u + 1)
                    for r in range(4):
                        t = pe.transpose(turn_bank[half][:, r * P:(r + 1) * P], mix[:, 4 * half + r, :], ident)
                    t.then_inc(m_turned[half], 1)
                for n, half_cols in ((2, slice(0, 2 * P)), (3, slice(2 * P, 4 * P))):
                    pe.matmul(lin_bank[1][:, half_cols], state[:, n - 2, :],
                              qg[:, n, :, :], start=n == 2, stop=False, skip_group_check=True)
                products = (
                    (0, slice(0, 4 * P), v_hi[:, 0, :], v_lo[:, 0, :], slice(0, 4)),
                    (1, slice(0, 2 * P), vmix_hi[:, :], vmix_lo[:, :], slice(4, 6)),
                    (1, slice(2 * P, 4 * P), v_hi[:, 1, :], v_lo[:, 1, :], slice(6, 8)))
                pe.wait_ge(v_lo_made, u + 1)
                pe.wait_ge(v_mixed, u + 1)
                for half, dst, a_hi, a_lo, rows in products:
                    pe.wait_ge(m_copied[half], u + 1)
                    pe.matmul(lin_bank[half][:, dst], a_hi, mT_hi[:, rows, :], start=half == 0, stop=False,
                              skip_group_check=True)
                    pe.matmul(lin_bank[half][:, dst], a_lo, mT_hi[:, rows, :], start=False, stop=False,
                              skip_group_check=True)
                if not last:
                    turn_kraw(u + 1)
                for i, (half, dst, a_hi, a_lo, rows) in enumerate(products):
                    pe.wait_ge(m_lo_made[half], u + 1)
                    mm = pe.matmul(lin_bank[half][:, dst], a_hi, mT_lo[:, rows, :], start=False, stop=i != 1,
                                   skip_group_check=True)
                    if i != 1:
                        mm.then_inc(pv_made[half], 1)

            over_units(pe, step)
            for tile in range(TT):
                pe.wait_ge(m_lo_made[tile], UNITS)
                turn_norm(2, tile)
            for tile in range(TT):
                pe.wait_ge(out_added[tile], UNITS - 1)
            output(UNITS - 1, B - 1, None)
            for tile in range(TT):
                pe.wait_ge(out_added[tile], UNITS)
            for i in range(TOK):
                if i + TT < TOK:
                    turn_norm(2, i + TT)
                ffn(TOK + i)

        @block.scalar
        def _(act):
            def root(r, i, n=1):
                act.wait_ge(eps_added[r], i + n)
                act.activation(dev[:, i:i + n], meanvar[:, i:i + n, 1], ACT.Sqrt).then_inc(dev_made[r], n)

            def copy_norm(r, i):
                act.wait_ge(xn_turned[r], i + 1)
                if r == 1:
                    act.wait_ge(ffn_made, i + 1)
                act.activation(xt_hi[:, :, i * P:(i + 1) * P],
                               norm_bank[r][i % 2][:, :].rearrange("p (k t) -> p k t", k=KT),
                               ACT.Copy).then_inc(xt_hi_made[r], 1)

            def split_chunk(g, k, par):
                act.wait_ge(w_in[k % 2], (g * 2 + (k // 2 + 1)) * 48)
                act.activation(w_hi[par][:, k, :], w_raw[k % 2][:, :], ACT.Copy).then_inc(w_hi_ready, 1)

            act.preload_act_table_set("sqrt_and_others")
            act.wait_ge(lb_turned, 1)
            act.activation(lbT, bank[0][0:R, :], ACT.Copy).then_inc(lb_copied, 1)
            for c in range(KT):
                act.wait_ge(eff_made, c + 1)
                if c >= 2:
                    act.wait_ge(squared, c - 1)
                act.activation(squares[c % 2], eff[c], ACT.Square, accum_out=norm2[:, c:c + 1]).then_inc(squared, 1)
            act.wait_ge(squared, KT)
            act.activation(colscale[:, :], norm2[:, :], ACT.Sqrt).then_inc(rooted, 1)
            root(0, 0, TOK // 2)
            split_chunk(0, 0, 0)
            split_chunk(0, 1, 0)
            act.wait_ge(fwt_turned, KT)
            for k in range(KT):
                if k == 2:
                    copy_norm(0, 0)
                act.activation(ff_hi[0][:, k, :], bank[k][:, :], ACT.Copy).then_inc(fw_hi_ready, 1)
            copy_norm(0, 1)
            for k in range(KT):
                act.wait_ge(fw_lo_ready, k + 1)
                act.activation(fwt[:, k, :], bank[k][:, :], ACT.Copy).then_inc(fwt_copied, 1)
            root(0, TOK // 2, TOK // 2)
            for i in range(2, TOK):
                copy_norm(0, i)
                root(1, i - 2)
                if i in (2, 3):
                    split_chunk(0, i, 0)
                if i >= 4:
                    copy_norm(1, i - 4)
            root(1, TOK - 2)
            copy_norm(1, TOK - 4)

            def split_wo(g, h):
                act.wait_ge(wo_in[h % 2], (g * 2 + (h // 2 + 1)) * 16)
                if not (isinstance(g, int) and g == 0):
                    act.wait_ge(out_made[1], g * B)
                act.activation(wo_hi[:, h, :], wo_raw[:, h % 2, :], ACT.Copy).then_inc(wo_hi_ready, 1)

            def copy_projected(u, upar, tile, first=False):
                act.wait_ge(q_made[tile], u + 1)
                if not first:
                    act.wait_ge(rotated[tile], u)
                    act.wait_ge(es_made[tile], u)
                act.activation(qk[tile][:, 0:GRP, :].rearrange("p h d -> p (h d)"), q_bank[:, :], ACT.Copy)\
                   .then_inc(q_copied[tile], 1)
                act.wait_ge(kv_made[tile], u + 1)
                if not first:
                    act.wait_ge(kraw_turned, u)
                act.activation(qk[tile][:, GRP, :], kv_bank[:, 0:D], ACT.Copy)
                if not (isinstance(u, int) and u < 2):
                    act.wait_ge(state_made, u - 1)
                    act.wait_ge(v_lo_made, u - 1)
                act.activation(v[upar][:, tile, :], kv_bank[:, D:2 * D], ACT.Copy).then_inc(kv_copied[tile], 1)

            def copy_kraw(u, first=False):
                act.wait_ge(kraw_turned, u + 1)
                if not first:
                    act.wait_ge(dec_made, u)
                act.activation(krawT[:, :], q_bank[:, 0:N], ACT.Copy).then_inc(kraw_copied, 1)

            def exp_projected(u, tile, first=False):
                act.wait_ge(max_made[tile], u + 1)
                act.wait_ge(q_copied[tile], u + 1)
                act.wait_ge(kv_copied[tile], u + 1)
                if not first:
                    act.wait_ge(es_turned[tile], u)
                    act.wait_ge(ks_turned, u)
                    act.wait_ge(es_recip[tile], u)
                for h in range(HEADS):
                    a = act.activation(es[tile][:, h, :], qk[tile][:, h, :], ACT.Exp, bias=nmax[tile][:, h:h + 1],
                                       accum_out=esum[tile][:, h:h + 1])
                a.then_inc(es_made[tile], 1)

            copy_projected(0, 0, 0, first=True)
            root(1, TOK - 1)
            copy_norm(1, TOK - 3)
            copy_projected(0, 0, 1, first=True)
            copy_kraw(0, first=True)
            act.preload_act_table_set("natural_log_exp_and_others")
            for i in range(TOK - TT, TOK):
                copy_norm(1, i)
            for tile in range(TT):
                exp_projected(0, tile, first=True)

            def step(g, b, first, last, odd=False, last_group=False):
                u = g * B + b
                par = int(odd)
                act.wait_ge(kr_turned, u + 1)
                if not first:
                    act.wait_ge(scored[1], u)
                act.activation(krT[:, :, :].rearrange("p (h t) w -> p t h w", t=TT),
                               kv_bank[:, 0:N].rearrange("p (t h w) -> p t h w", t=TT, w=W), ACT.Copy)\
                   .then_inc(kr_copied, 1)
                act.wait_ge(abs_made, u + 1)
                act.activation(lnk[:, :], lnk[:, :], ACT.Exp).then_inc(kexp_made, 1)
                for tile in range(TT):
                    act.wait_ge(qr_turned[tile], u + 1)
                    if not first:
                        act.wait_ge(scored[tile], u)
                    act.activation(qrT[:, 2 * tile:2 * tile + 2, :, :].rearrange("p n h t -> p h n t"),
                                   turn_bank[tile][:, :].rearrange("p (h n t) -> p h n t", h=GRP, n=2), ACT.Copy)\
                       .then_inc(qr_copied[tile], 1)
                    if tile == 0:
                        act.wait_ge(kexp_made, u + 1)
                        act.activation(lnk[:, :], lnk[:, :], ACT.Ln, bias=1.0).then_inc(kln_made, 1)
                if b == 1:
                    split_wo(g, 2)
                if not last:
                    copy_projected(u + 1, (b + 1) % 2, 0)
                if b == 1:
                    split_wo(g, 3)
                act.wait_ge(dec_bounded, u + 1)
                act.activation(dec[:, :], dec[:, :], ACT.Exp, scale=1.0 / GATE_NORM).then_inc(gates_made, 1)
                act.wait_ge(kv_copied[0], u + 1)
                act.wait_ge(kv_copied[1], u + 1)
                if not first:
                    act.wait_ge(pv_made[1], u)
                    act.wait_ge(v_mixed, u)
                act.activation(v_hi[:, :, :], v[b % 2][:, :, :], ACT.Copy).then_inc(v_hi_made, 1)
                act.wait_ge(ks_turned, u + 1)
                if not first:
                    act.wait_ge(kg_made, u)
                act.activation(ksT[:, :], kv_bank[:, 0:N], ACT.Copy).then_inc(ks_copied, 1)
                if not last:
                    exp_projected(u + 1, 0)
                for half in range(2):
                    act.wait_ge(masked[half], u + 1)
                    for r in range(4 * half, 4 * half + 4):
                        seen = slice(0, WIN_COLS[r // 2])
                        a = act.activation(sc[:, r, seen], sc[:, r, seen], ACT.Exp, scale=-1.0, bias=scmin[:, r:r + 1],
                                           accum_out=ssum[:, r:r + 1])
                    a.then_inc(e_made[half], 1)
                if last:
                    root(2, 0, TT)
                else:
                    copy_projected(u + 1, (b + 1) % 2, 1)
                act.wait_ge(k2_turned, u + 1)
                if not first:
                    act.wait_ge(state_made, u)
                act.activation(k2[:, :], turn_bank[0][:, 0:D], ACT.Copy).then_inc(k2_copied, 1)
                if last_group:
                    act.activation(ff_hi[1][:, b, :], fwt[:, b, :], ACT.Copy).then_inc(fw_hi_ready, 1)
                else:
                    for k in SPLIT_AT[b]:
                        split_chunk(g + 1, k, 1 - par)
                act.wait_ge(state_made, u + 1)
                act.wait_ge(gates_made, u + 1)
                if not first:
                    act.wait_ge(pv_made[1], u)
                act.activation(state[:, 0, :], turn_bank[1][:, 0:D], ACT.Copy)
                act.activation(state[:, 1, :], turn_bank[1][:, 0:D], ACT.Copy, scale=dec[:, DSTEP:DSTEP + 1])\
                   .then_inc(state_copied, 1)
                if b == 0:
                    split_wo(g, 0)
                for half in range(2):
                    act.wait_ge(m_turned[half], u + 1)
                    if not first:
                        act.wait_ge(pv_made[half], u)
                    act.activation(mT_hi[:, 4 * half:4 * half + 4, :].rearrange("p r q -> p (r q)"), turn_bank[half][:, :],
                                   ACT.Copy).then_inc(m_copied[half], 1)
                if last:
                    root(2, TT, TT)
                else:
                    exp_projected(u + 1, 1)
                    copy_kraw(u + 1)
                for half in range(2):
                    act.wait_ge(pv_made[half], u + 1)
                    if not first:
                        act.wait_ge(o_ready[half], u)
                    act.activation(o_bf[:, half, :, :].rearrange("p h (n t) -> p h n t", n=2),
                                   lin_bank[half][:, :].rearrange("p (n h t) -> p h n t", n=2, h=GRP),
                                   ACT.Copy, scale=0.5).then_inc(o_copied[half], 1)
                if b == 0:
                    split_wo(g, 1)

            over_units(act, step)
            for i in range(TOK):
                if i == TT:
                    root(2, TOK - 2 * TT, TT)
                    for tile in range(TT):
                        root(2, TOK - TT + tile)
                copy_norm(2, i)

        @block.vector
        def _(dve):
            def statistics(r, i):
                if r == 0:
                    dve.wait_ge(x_in[i], 16)
                elif r == 1:
                    dve.wait_ge(ffn_added, i + 1)
                else:
                    dve.wait_ge(out_added[i % TT], UNITS - B + i // TT + 1)
                dve.bn_stats(stat[:, i, :], x[:, i, :]).then_inc(stats_made[r], 1)
                dve.wait_ge(stats_made[r], i + 1)
                if r >= 1:
                    dve.wait_ge(xn_made[r - 1], i + 1)
                dve.bn_aggr(meanvar[:, i, :], stat[:, i, :]).then_inc(aggregated[r], 1)
                dve.wait_ge(aggregated[r], i + 1)
                dve.tensor_scalar(meanvar[:, i, 1:2], meanvar[:, i, 1:2], EPS, None, ALU.add).then_inc(eps_added[r], 1)

            def invert_dev(r, i, n=1):
                dve.wait_ge(dev_made[r], i + n)
                dve.reciprocal(rstd[:, i:i + n], dev[:, i:i + n]).then_inc(rstd_made[r], n)

            def normalise(r, i):
                dve.wait_ge(rstd_made[r], i + 1)
                if i >= 2:
                    dve.wait_ge(xn_turned[r], i - 1)
                dve.tensor_scalar(xn[r % 2][i % 2], x[:, i, :], meanvar[:, i, 0:1], rstd[:, i:i + 1],
                                  ALU.subtract, ALU.mult).then_inc(xn_made[r], 1)

            def rest_norm(r, i):
                cols = slice(i * P, (i + 1) * P)
                dve.wait_ge(xt_hi_made[r], i + 1)
                dve.tensor_tensor(xt_lo[:, :, cols], norm_bank[r][i % 2][:, :].rearrange("p (k t) -> p k t", k=KT),
                                  xt_hi[:, :, cols].bitcast(F32), ALU.subtract).then_inc(xt_lo_made[r], 1)

            def add_ffn(f):
                dve.wait_ge(ffn_made, f + 1)
                dve.tensor_tensor(x[:, f % TOK, :], score_bank[f % 2][:, :], x[:, f % TOK, :], ALU.add)\
                   .then_inc(ffn_added, 1)

            dve.wait_ge(fw_in, 32)
            for c in range(KT):
                dve.wait_ge(ba_made, c + 1)
                dve.tensor_tensor(eff[c], bank[4 + c][:, :], fwt[:, c, :], ALU.add).then_inc(eff_made, 1)
                statistics(0, c)
            dve.wait_ge(rooted, 1)
            dve.reciprocal(norm2[:, :], colscale[:, :]).then_inc(scaled_c, 1)
            dve.wait_ge(scaled_c, 1)
            dve.scalar_tensor_tensor(out=colscale[:, :], in0=norm2[:, :], scalar=0.5, in1=magc[:, :],
                                     op0=ALU.mult, op1=ALU.mult).then_inc(scaled_c, 1)
            dve.wait_ge(scaled_c, 2)
            for c in range(KT):
                dve.tensor_scalar(eff[c], eff[c], colscale[:, c:c + 1], None, ALU.mult).then_inc(eff_scaled, 1)
            invert_dev(0, 0, TOK // 2)
            normalise(0, 0)
            normalise(0, 1)
            statistics(0, 4)
            statistics(0, 5)
            for k in range(KT):
                if k == 2:
                    rest_norm(0, 0)
                dve.wait_ge(fw_hi_ready, k + 1)
                dve.tensor_tensor(ff_lo[0][:, k, :], bank[k][:, :], ff_hi[0][:, k, :].bitcast(F32), ALU.subtract)\
                   .then_inc(fw_lo_ready, 1)
            rest_norm(0, 1)
            statistics(0, 6)
            statistics(0, 7)
            invert_dev(0, TOK // 2, TOK // 2)

            def after_ffn(i, rest=None):
                add_ffn(i)
                statistics(1, i)
                if rest is not None:
                    rest_norm(0, rest)
                invert_dev(1, i)
                normalise(1, i)

            for i in range(2, TOK):
                after_ffn(i - 2, rest=i)
                if i >= 4:
                    rest_norm(1, i - 4)
            after_ffn(TOK - 2)
            rest_norm(1, TOK - 4)

            def prepare(u, tile, first=False):
                dve.wait_ge(q_copied[tile], u + 1)
                dve.wait_ge(kv_copied[tile], u + 1)
                if not first:
                    dve.wait_ge(roped[tile], u)
                    dve.wait_ge(kr_turned, u)
                    dve.wait_ge(qr_turned[tile], u)
                dve.tensor_tensor(rc[tile][:, :, :], qk[tile][:, :, :],
                                  cos[:, tile, :].unsqueeze(1).to_broadcast([P, HEADS, D]), ALU.mult)
                for a, b in ((0, D // 2), (D // 2, 0)):
                    r = dve.tensor_tensor(rs[tile][:, :, a:a + D // 2], qk[tile][:, :, b:b + D // 2],
                                          sin[:, tile, a:a + D // 2].unsqueeze(1).to_broadcast([P, HEADS, D // 2]),
                                          ALU.mult)
                r.then_inc(rotated[tile], 1)
                if not first:
                    dve.wait_ge(es_made[tile], u)
                dve.tensor_reduce(nmax[tile][:, :], qk[tile][:, :, :], AX_X, ALU.max, negate=True)\
                   .then_inc(max_made[tile], 1)

            def invert(u, tile, first=False):
                dve.wait_ge(es_made[tile], u + 1)
                if not first:
                    dve.wait_ge(es_scaled[tile], u)
                dve.reciprocal(erec[tile][:, :], esum[tile][:, :]).then_inc(es_recip[tile], 1)

            def mask_scores(u, half):
                dve.wait_ge(scored[half], u + 1)
                dve.nop(nofuse=True)
                for r in range(4 * half, 4 * half + 4):
                    seen = WIN_COLS[r // 2]
                    m = dve.tensor_tensor_reduce(sc[:, r, 0:seen], score_bank[half][:, (r % 4) * P:(r % 4) * P + seen],
                                                 win[:, WIN_OF_BLOCK[r // 2], 0:seen], -float(D) ** -0.5, BIG,
                                                 ALU.add, ALU.min, scmin[:, r:r + 1])
                m.then_inc(masked[half], 1)

            def add_output(u, b):
                for tile in range(TT):
                    i = b * TT + tile
                    dve.wait_ge(out_made[tile], u + 1)
                    dve.tensor_tensor(x[:, i, :], score_bank[tile][:, :], x[:, i, :], ALU.add).then_inc(out_added[tile], 1)

            dve.wait_ge(ident_in, 16)
            dve.wait_ge(tables_in, 16)
            prepare(0, 0, first=True)
            after_ffn(TOK - 1)
            rest_norm(1, TOK - 3)
            prepare(0, 1, first=True)
            for i in range(TOK - TT, TOK):
                rest_norm(1, i)
            for tile in range(TT):
                invert(0, tile, first=True)
            dve.memset(mix[:, 0:2, W:P], 0.0)

            def step(g, b, first, last, odd=False, last_group=False):
                u = g * B + b
                dve.wait_ge(kraw_copied, u + 1)
                dve.scalar_tensor_tensor(out=lnk[:, :], in0=krawT[:, :], scalar=-1.0, in1=krawT[:, :],
                                         op0=ALU.mult, op1=ALU.min).then_inc(abs_made, 1)
                dve.wait_ge(kln_made, u + 1)
                dve.scalar_tensor_tensor(out=lnk[:, :], in0=krawT[:, :], scalar=0.0, in1=lnk[:, :],
                                         op0=ALU.min, op1=ALU.subtract).then_inc(logs_made, 1)
                dve.wait_ge(logs_made, u + 1)
                dve.tensor_tensor_scan(G[:, :], ones, lnk[:, :], 0.0, ALU.mult, ALU.add).then_inc(summed, 1)
                dve.wait_ge(summed, u + 1)
                if not first:
                    dve.wait_ge(state_copied, u)
                mid = G[:, W // 2 - 1::W]
                dve.tensor_tensor(dec[:, 0:3 * P].rearrange("p (n s) -> p n s", n=3),
                                  mid[:, 0:3].unsqueeze(2).to_broadcast([P, 3, P]),
                                  G[:, 0:P].unsqueeze(1).to_broadcast([P, 3, P]), ALU.subtract)
                dve.tensor_tensor(dec[:, 3 * P:5 * P].rearrange("p (n s) -> p n s", n=2),
                                  mid[:, 2:4].unsqueeze(2).to_broadcast([P, 2, P]),
                                  G[:, P:2 * P].unsqueeze(1).to_broadcast([P, 2, P]), ALU.subtract)
                dve.tensor_tensor(dec[:, DQ:DSTEP].rearrange("p (n s) -> p n s", n=NB),
                                  G[:, :].rearrange("p (n s) -> p n s", n=NB),
                                  mid.unsqueeze(2).to_broadcast([P, NB, W]), ALU.subtract)
                dve.tensor_tensor(dec[:, DSTEP:DSTEP + 1], mid[:, 3:4], mid[:, 2:3], ALU.subtract).then_inc(dec_made, 1)
                dve.wait_ge(dec_made, u + 1)
                dve.tensor_scalar(dec[:, :], dec[:, :], MOST, None, ALU.min).then_inc(dec_bounded, 1)
                if not last:
                    prepare(u + 1, 0)
                mask_scores(u, 0)
                if last:
                    mask_scores(u, 1)
                dve.wait_ge(gates_made, u + 1)
                for tile in range(TT):
                    dve.wait_ge(es_turned[tile], u + 1)
                    if not first:
                        dve.wait_ge(lin_made[tile], u)
                        dve.wait_ge(pv_made[1], u)
                    dve.tensor_tensor(qg[:, 2 * tile:2 * tile + 2, :, :].rearrange("p n h t -> p h n t"),
                                      turn_bank[tile][:, :].rearrange("p (h n t) -> p h n t", h=GRP, n=2),
                                      dec[:, DQ + tile * P:DQ + (tile + 1) * P].rearrange("p (n t) -> p n t", n=2)
                                      .unsqueeze(1).to_broadcast([P, GRP, 2, W]),
                                      ALU.mult).then_inc(qg_made[tile], 1)
                dve.wait_ge(ks_copied, u + 1)
                if not first:
                    dve.wait_ge(lin_made[1], u)
                    dve.wait_ge(k2_turned, u)
                dve.tensor_tensor(kg[:, 0:3, :], ksT[:, 0:P].unsqueeze(1).to_broadcast([P, 3, P]),
                                  dec[:, 0:3 * P].rearrange("p (n s) -> p n s", n=3), ALU.mult)
                dve.tensor_tensor(kg[:, 3:5, :], ksT[:, P:2 * P].unsqueeze(1).to_broadcast([P, 2, P]),
                                  dec[:, 3 * P:5 * P].rearrange("p (n s) -> p n s", n=2), ALU.mult).then_inc(kg_made, 1)
                if not last:
                    mask_scores(u, 1)
                dve.wait_ge(v_lo_made, u + 1)
                if not first:
                    dve.wait_ge(pv_made[1], u)
                for dst, src in ((vmix_hi, v_hi), (vmix_lo, v_lo)):
                    dve.tensor_copy(dst[0:W, :], src[0:W, 1, :])
                    c = dve.tensor_copy(dst[W:P, :], src[W:P, 0, :])
                c.then_inc(v_mixed, 1)
                if last:
                    statistics(2, 0)
                    statistics(2, 1)
                if not last:
                    invert(u + 1, 0)
                for half in range(2):
                    rows = slice(4 * half, 4 * half + 4)
                    dve.wait_ge(e_made[half], u + 1)
                    dve.reciprocal(srec[:, rows], ssum[:, rows]).then_inc(e_recip[half], 1)
                    dve.wait_ge(lin_made[half], u + 1)
                    if not first:
                        dve.wait_ge(m_turned[half], u)
                    for n in (2 * half, 2 * half + 1):
                        seen, col = LIN_COLS[n], (n % 2) * 2 * P
                        m = dve.tensor_tensor(mix[:, 2 * n:2 * n + 2, 0:seen],
                                              lin_bank[half][:, col:col + 2 * P].rearrange("p (h k) -> p h k", h=2)[:, :, 0:seen],
                                              lin[:, n % 2, 0:seen].unsqueeze(1).to_broadcast([P, 2, seen]), ALU.min)
                    m.then_inc(lin_masked[half], 1)
                    dve.wait_ge(e_recip[half], u + 1)
                    dve.wait_ge(lin_masked[half], u + 1)
                    for r in range(4 * half, 4 * half + 4):
                        both, seen = LIN_COLS[r // 2], WIN_COLS[r // 2]
                        m = dve.scalar_tensor_tensor(out=mix[:, r, 0:both], in0=sc[:, r, 0:both], scalar=srec[:, r:r + 1],
                                                     in1=mix[:, r, 0:both], op0=ALU.mult, op1=ALU.add)
                        if both < seen:
                            dve.tensor_scalar(mix[:, r, both:seen], sc[:, r, both:seen], srec[:, r:r + 1], None, ALU.mult)
                    m.then_inc(mixed[half], 1)
                if not last:
                    prepare(u + 1, 1)
                if last:
                    statistics(2, 2)
                    statistics(2, 3)
                for half in range(2):
                    rows = slice(4 * half, 4 * half + 4)
                    dve.wait_ge(m_copied[half], u + 1)
                    if not first:
                        dve.wait_ge(pv_made[half], u)
                    dve.tensor_tensor(mT_lo[:, rows, :].rearrange("p r q -> p (r q)"), turn_bank[half][:, :],
                                      mT_hi[:, rows, :].rearrange("p r q -> p (r q)").bitcast(F32), ALU.subtract)\
                       .then_inc(m_lo_made[half], 1)
                if last:
                    invert_dev(2, 0, TT)
                    invert_dev(2, TT, TT)
                    for tile in range(TT):
                        normalise(2, tile)
                if not first:
                    add_output(u - 1, (b - 1) % B)
                if last:
                    for tile in range(TT):
                        statistics(2, (b - 1) * TT + tile)
                if not last:
                    invert(u + 1, 1)

            over_units(dve, step)
            for tile in range(TT):
                rest_norm(2, tile)
                normalise(2, TT + tile)
            add_output(UNITS - 1, B - 1)
            for tile in range(TT):
                statistics(2, TOK - TT + tile)
            for i in range(TT, TOK + 1):
                if i < TOK:
                    rest_norm(2, i)
                if i == TT:
                    invert_dev(2, TOK - 2 * TT, TT)
                    for tile in range(TT):
                        invert_dev(2, TOK - TT + tile)
                if i + TT < TOK:
                    normalise(2, i + TT)
                add_ffn(TOK + i - TT)
            add_ffn(2 * TOK - 1)

        @block.gpsimd
        def _(pool):
            def split_chunk(g, k, par):
                pool.wait_ge(w_hi_ready, g * KT + (k + 1))
                pool.tensor_tensor(w_lo[par][:, k, :], w_raw[k % 2][:, :], w_hi[par][:, k, :].bitcast(F32), ALU.subtract)\
                    .then_inc(w_lo_ready, 1)

            def split_wo(g, h):
                pool.wait_ge(wo_hi_ready, g * GRP + (h + 1))
                pool.tensor_tensor(wo_lo[:, h, :], wo_raw[:, h % 2, :], wo_hi[:, h, :].bitcast(F32), ALU.subtract)\
                    .then_inc(wo_lo_ready, 1)

            def rope(u, tile):
                pool.wait_ge(rotated[tile], u + 1)
                pool.tensor_tensor(rc[tile][:, :, :], rc[tile][:, :, :], rs[tile][:, :, :], ALU.add)\
                    .then_inc(roped[tile], 1)

            def scale(u, tile):
                pool.wait_ge(es_recip[tile], u + 1)
                pool.tensor_tensor(es[tile][:, :, :], es[tile][:, :, :],
                                   erec[tile][:, :].unsqueeze(2).to_broadcast([P, HEADS, D]), ALU.mult)\
                    .then_inc(es_scaled[tile], 1)

            split_chunk(0, 0, 0)
            split_chunk(0, 1, 0)
            for i in range(2, TOK):
                pool.wait_ge(rstd_made[0], TOK // 2 if i < TOK // 2 else TOK)
                pool.wait_ge(xn_made[0], i)
                pool.wait_ge(xn_turned[0], i - 1)
                pool.tensor_scalar(xn[0][i % 2], x[:, i, :], meanvar[:, i, 0:1], rstd[:, i:i + 1],
                                   ALU.subtract, ALU.mult).then_inc(xn_made[0], 1)
                if i in (4, 5):
                    split_chunk(0, i - 2, 0)
            for tile in range(TT):
                rope(0, tile)
            for tile in range(TT):
                scale(0, tile)

            def step(g, b, first, last, odd=False, last_group=False):
                u = g * B + b
                par = int(odd)
                if not last:
                    rope(u + 1, 0)
                pool.wait_ge(v_hi_made, u + 1)
                if not first:
                    pool.wait_ge(pv_made[1], u)
                    pool.wait_ge(v_mixed, u)
                pool.tensor_tensor(v_lo[:, :, :], v[b % 2][:, :, :], v_hi[:, :, :].bitcast(F32), ALU.subtract)\
                    .then_inc(v_lo_made, 1)
                if b == 1:
                    split_wo(g, 2)
                    split_wo(g, 3)
                if not last:
                    scale(u + 1, 0)
                if not last_group:
                    for k in SPLIT_AT[b]:
                        split_chunk(g + 1, k, 1 - par)
                if not last:
                    rope(u + 1, 1)
                if b == 0:
                    split_wo(g, 0)
                if not last:
                    scale(u + 1, 1)
                if b == 0:
                    split_wo(g, 1)
                for half in range(2):
                    pool.wait_ge(o_copied[half], u + 1)
                    if not first:
                        pool.wait_ge(out_made[half], u)
                    pool.nop(nofuse=True)
                    pool.tensor_copy(o_r[:, half, :, :], o_bf[:, half, :, :]).then_inc(o_ready[half], 1)
                if last_group:
                    pool.wait_ge(fw_hi_ready, KT + b + 1)
                    pool.tensor_tensor(ff_lo[1][:, b, :], fwt[:, b, :], ff_hi[1][:, b, :].bitcast(F32), ALU.subtract)\
                        .then_inc(fw_lo_ready, 1)

            over_units(pool, step)


def shape_constants():
    import numpy as np
    c = np.zeros((P, C_ALL), np.float32)
    half = np.arange(D // 2, dtype=np.float32)
    inv = np.float32(1.0) / np.power(np.float32(10000.0), np.float32(2.0) * half / np.float32(D))
    fr = np.arange(N, dtype=np.float32)[:, None] * inv[None, :].astype(np.float32)
    cos, sin = np.cos(fr), np.sin(fr)
    for t in range(TT):
        rows = slice(t * P, (t + 1) * P)
        c[:, C_COS + t * D:C_COS + (t + 1) * D] = np.concatenate([cos[rows], cos[rows]], 1)
        c[:, C_SIN + t * D:C_SIN + (t + 1) * D] = np.concatenate([-sin[rows], sin[rows]], 1)
    t = np.arange(P)[:, None] % W
    k = np.arange(P)[None, :]
    own, back = k % W <= t, k % W >= t
    early = k < W
    windows = (early & own, (early & back) | (~early & own), (early & own) | (~early & back))
    for i, seen in enumerate(windows):
        c[:, C_WIN + i * P:C_WIN + (i + 1) * P] = np.where(seen, 0.0, FAR)
    for i, seen in enumerate((early & own, early | own)):
        c[:, C_LIN + i * P:C_LIN + (i + 1) * P] = np.where(seen, BIG, 0.0)
    c[:, C_ID:C_ONE] = np.eye(P)
    c[:, C_ONE] = 1.0
    return c


def kernel(L0_attn_hidden_states, L0_attn_Wq, L0_attn_Wk, L0_attn_Wv, L0_attn_Wo, L0_ffn_W, L0_ffn_lora_A,
           L0_ffn_lora_B, L0_ffn_magnitude):
    import numpy as np
    import concourse.bacc as bacc
    from concourse.bass_utils import run_bass_kernel_spmd

    nc = bacc.Bacc("TRN2", target_bir_lowering=False, num_devices=1)
    arrays = {
        "hs": np.ascontiguousarray(L0_attn_hidden_states).reshape(B * N, HID),
        "wq": L0_attn_Wq, "wk": L0_attn_Wk, "wv": L0_attn_Wv, "wo": L0_attn_Wo,
        "fw": L0_ffn_W, "la": L0_ffn_lora_A, "lb": L0_ffn_lora_B,
        "mag": np.asarray(L0_ffn_magnitude).reshape(KT, P).T,
        "consts": shape_constants(),
    }
    arrays = {f"{name}_dram": np.ascontiguousarray(a) for name, a in arrays.items()}
    args = [nc.dram_tensor(name, a.shape, mybir.dt.from_np(a.dtype), kind="ExternalInput").ap()
            for name, a in arrays.items()]
    args.append(nc.dram_tensor("out_dram", (B * N, HID), F32, kind="ExternalOutput").ap())
    layer_program(nc, *args)
    r = run_bass_kernel_spmd(nc, [arrays], core_ids=[0])
    return r.results[0]["out_dram"].reshape(B, N, HID)
```
